# Optimizing a Trainium2 kernel written in Bass

```python
import numpy as np
import jax
import jax.numpy as jnp

def _softmax(x, axis=-1):
    return jax.nn.softmax(x, axis=axis)

def _gelu(x):
    return jax.nn.gelu(x, approximate=True)

def _silu(x):
    return jax.nn.silu(x)

def _sigmoid(x):
    return jax.nn.sigmoid(x)

def _layernorm(x, axis=-1, eps=1e-05):
    m = jnp.mean(x, axis=axis, keepdims=True)
    v = jnp.var(x, axis=axis, keepdims=True)
    return (x - m) / jnp.sqrt(v + eps)

def _scatter_add(tgt, idx, src, axis=0):
    return tgt.at[idx].add(src)

def _segment_sum(src, seg, n):
    return jax.ops.segment_sum(src, seg, n)
kernel_name = 'mk_lm_tower_d1_tok_ids1024_r4_347945'

def setup_inputs(seed: int=0):
    np.random.seed(seed)
    _w = jnp.asarray

    def _rec_inputs():
        import jax
        import jax.numpy as jnp
        _rk = jax.random.key(seed)
        x = jax.random.randint(jax.random.fold_in(_rk, 1), (64, 256), 0, 131066, jnp.int32)
        return x
    x = _rec_inputs()

    def _L0_tok_setup():
        import jax, jax.numpy as jnp
        import numpy as np
        BATCH, SEQ = (4, 1024)
        VOCAB, HIDDEN = (32768, 256)
        key = jax.random.key(seed)
        k_ids, k_tab = jax.random.split(key)
        input_ids = jax.random.randint(k_ids, (BATCH, SEQ), 0, VOCAB, dtype=jnp.int64)
        embed_table = jax.random.normal(k_tab, (VOCAB, HIDDEN), dtype=jnp.float32) * 0.02
        return {'input_ids': input_ids, 'embed_table': embed_table}
    _L0_tok_all = _L0_tok_setup()
    _L0_tok_in = {k: v for k, v in _L0_tok_all.items() if k in ('embed_table',)}
    del _L0_tok_all

    def _L0_attn_setup():
        import jax, jax.numpy as jnp
        import numpy as np
        B, T, D = (8, 1024, 256)

        def log_g(x):
            return jnp.where(x >= 0, jnp.log(jnp.maximum(x, 0) + 0.5), -jax.nn.softplus(-x))
        key = jax.random.key(seed)
        kx, kf, ki, kh = jax.random.split(key, 4)
        s = 1.0 / np.sqrt(D).astype(np.float32)
        return {'x': jax.random.normal(kx, (B, T, D), dtype=jnp.float32), 'Wf': jax.random.normal(kf, (D, D), dtype=jnp.float32) * s, 'Wi': jax.random.normal(ki, (D, D), dtype=jnp.float32) * s, 'Wh': jax.random.normal(kh, (D, D), dtype=jnp.float32) * s}
    _L0_attn_all = _L0_attn_setup()
    _L0_attn_in = {k: v for k, v in _L0_attn_all.items() if k in ('Wf', 'Wi', 'Wh')}
    del _L0_attn_all

    def _L0_ffn_setup():
        import jax, jax.numpy as jnp
        import numpy as np

        def _bitlinear(x, w_latent):
            scale = jax.lax.stop_gradient(jnp.clip(jnp.mean(jnp.abs(w_latent), axis=1, keepdims=True), 1e-05, None))
            tern = jnp.clip(jnp.round(w_latent / scale), -1.0, 1.0)
            w = w_latent + jax.lax.stop_gradient(tern - w_latent)
            return x @ (w * scale).T
        key = jax.random.key(seed)
        ks = jax.random.split(key, 6)
        dim, hidden, rank = (256, 1024, 16)
        B, S = (4, 1024)
        x = jax.random.normal(ks[0], (B, S, dim), dtype=jnp.float32)
        w_fc = 0.02 * jax.random.normal(ks[1], (hidden, dim), dtype=jnp.float32)
        w_proj = 0.02 * jax.random.normal(ks[2], (dim, hidden), dtype=jnp.float32)
        u = 0.02 * jax.random.normal(ks[3], (hidden, rank), dtype=jnp.float32)
        v = 0.02 * jax.random.normal(ks[4], (rank, dim), dtype=jnp.float32)
        fast_b = jax.random.normal(ks[5], (rank, rank), dtype=jnp.float32)
        gate = jnp.float32(0.05)
        return {'x': x, 'fast_b': fast_b, 'w_fc': w_fc, 'w_proj': w_proj, 'u': u, 'v': v, 'gate': gate}
    _L0_ffn_all = _L0_ffn_setup()
    _L0_ffn_in = {k: v for k, v in _L0_ffn_all.items() if k in ('fast_b', 'w_fc', 'w_proj', 'u', 'v', 'gate')}
    del _L0_ffn_all
    return {'x': x, 'L0_tok_embed_table': _L0_tok_in['embed_table'], 'L0_attn_Wf': _L0_attn_in['Wf'], 'L0_attn_Wi': _L0_attn_in['Wi'], 'L0_attn_Wh': _L0_attn_in['Wh'], 'L0_ffn_fast_b': _L0_ffn_in['fast_b'], 'L0_ffn_w_fc': _L0_ffn_in['w_fc'], 'L0_ffn_w_proj': _L0_ffn_in['w_proj'], 'L0_ffn_u': _L0_ffn_in['u'], 'L0_ffn_v': _L0_ffn_in['v'], 'L0_ffn_gate': _L0_ffn_in['gate']}

def reference(x, L0_tok_embed_table, L0_attn_Wf, L0_attn_Wi, L0_attn_Wh, L0_ffn_fast_b, L0_ffn_w_fc, L0_ffn_w_proj, L0_ffn_u, L0_ffn_v, L0_ffn_gate):
    import jax
    import jax.numpy as jnp

    def _L0_tok_ref(input_ids, embed_table):
        import jax, jax.numpy as jnp
        import numpy as np
        BATCH, SEQ = (4, 1024)
        VOCAB, HIDDEN = (32768, 256)
        hidden_states = jnp.take(embed_table, input_ids, axis=0)
        return jnp.nan_to_num(hidden_states, nan=0.0)

    def _L0_attn_ref(x, Wf, Wi, Wh):
        import jax, jax.numpy as jnp
        import numpy as np
        B, T, D = (8, 1024, 256)

        def log_g(x):
            return jnp.where(x >= 0, jnp.log(jnp.maximum(x, 0) + 0.5), -jax.nn.softplus(-x))
        log_f = jax.nn.log_sigmoid(jnp.einsum('btd,ed->bte', x, Wf))
        log_i = jax.nn.log_sigmoid(jnp.einsum('btd,ed->bte', x, Wi))
        log_tilde_h = log_g(jnp.einsum('btd,ed->bte', x, Wh))
        b, t, d = x.shape
        log_h0 = jnp.full((b, 1, d), jnp.log(jnp.float32(0.5)), dtype=x.dtype)
        log_values = jnp.concatenate([log_h0, log_i + log_tilde_h], axis=1)
        a_star = jnp.concatenate([jnp.zeros((b, 1, d), x.dtype), jnp.cumsum(log_f, axis=1)], axis=1)
        log_h0_plus_b_star = jax.lax.associative_scan(jnp.logaddexp, log_values - a_star, axis=1)
        log_h = a_star + log_h0_plus_b_star
        return jnp.exp(log_h)[:, 1:]

    def _L0_ffn_ref(x, fast_b, w_fc, w_proj, u, v, gate):
        import jax, jax.numpy as jnp
        import numpy as np

        def _bitlinear(x, w_latent):
            scale = jax.lax.stop_gradient(jnp.clip(jnp.mean(jnp.abs(w_latent), axis=1, keepdims=True), 1e-05, None))
            tern = jnp.clip(jnp.round(w_latent / scale), -1.0, 1.0)
            w = w_latent + jax.lax.stop_gradient(tern - w_latent)
            return x @ (w * scale).T
        h = _bitlinear(x, w_fc) + gate * (x @ v.T @ fast_b.T @ u.T)
        r = jnp.maximum(h, 0.0)
        return _bitlinear(r * r, w_proj)
    h = _L0_tok_ref(x, L0_tok_embed_table)
    h = h + _L0_attn_ref(_layernorm(h, axis=-1), L0_attn_Wf, L0_attn_Wi, L0_attn_Wh)
    h = h + _L0_ffn_ref(_layernorm(h, axis=-1), L0_ffn_fast_b, L0_ffn_w_fc, L0_ffn_w_proj, L0_ffn_u, L0_ffn_v, L0_ffn_gate)
    return h

_drawn_inputs = setup_inputs


def setup_inputs(seed=0):
    import zlib

    import numpy as np

    out = dict(_drawn_inputs(seed))
    spreads = {}
    factors = {'L0_ffn_fast_b': 8.0, 'L0_ffn_u': 8.0, 'L0_ffn_v': 8.0}
    for name, (base, spread) in spreads.items():
        noise = np.random.default_rng([zlib.crc32(name.encode()), seed]).standard_normal(out[name].shape)
        drawn = base * np.exp(spread * noise) if base else spread * noise
        out[name] = jnp.asarray(drawn.astype(out[name].dtype))
    for name, factor in factors.items():
        out[name] = (out[name] * factor).astype(out[name].dtype)
    return out
```

```python
from contextlib import ExitStack

import concourse.bass as bass
from concourse import mybir

ALU = mybir.AluOpType
ACT = mybir.ActivationFunctionType
AX = mybir.AxisListType.X
F32 = mybir.dt.float32
F16 = mybir.dt.float16
BF16 = mybir.dt.bfloat16
I32 = mybir.dt.int32

P = 128
SEQS, T = 64, 256
D = 256
V = 32768
HID = 1024
R = 16
CHUNK = 512
N = SEQS * T // CHUNK
TILES = CHUNK // P
KD = D // P
FC = HID // P
EPS = 1e-5
FMAX = 3.4028234663852886e38
EXPONENT = 0x7F800000
W_TOP = 2.0 ** 10
LOW_TOP = 2.0 ** 10
RELU_TOP = 2.0 ** 6

FIRST_LOOP, LAST_LOOP = 3, N - 4


def build(nc, ids, table, wf, wi, wh, fast_b, w_fc, w_proj, u, v, gate, out):
    ctx = ExitStack()
    with ctx:
        def sb(name, shape, dt=F32):
            return ctx.enter_context(nc.sbuf_tensor(name, shape, dt))

        def sem(name):
            return ctx.enter_context(nc.semaphore(name))

        ident = sb("ident", [P, P])
        w_hi = sb("w_hi", [P, KD, 6, P], F16)
        w_lo = sb("w_lo", [P, KD, 6, P], F16)
        w_back = sb("w_back", [P, 6])
        fc_t = sb("fc_t", [P, KD, HID], BF16)
        low_a = sb("low_a", [P, KD, P], F16)
        low_u = sb("low_u", [P, HID], F16)
        relu_scale = sb("relu_scale", [P, FC])
        proj_t = sb("proj_t", [P, FC, D], BF16)
        proj_scale = sb("proj_scale", [P, D])
        minus_half = sb("minus_half", [P, TILES])
        idx_all = sb("idx_all", [P, N * TILES], I32)

        idx_now = sb("idx_now", [P, 2, TILES], I32)
        rows_raw = sb("rows_raw", [P, 2, TILES, D])
        rows_pos = sb("rows_pos", [P, TILES, D])
        rows_neg = sb("rows_neg", [P, TILES, D])
        h0 = sb("h0", [P, 2, TILES, D])
        h1 = sb("h1", [P, 2, TILES, D])
        stats = [sb(f"stats{k}", [P, TILES, 6]) for k in range(2)]
        moments = [sb(f"moments{k}", [P, TILES, 2]) for k in range(2)]
        var_eps = [sb(f"var_eps{k}", [P, TILES]) for k in range(2)]
        rstd = [sb(f"rstd{k}", [P, TILES]) for k in range(2)]
        normed = [sb(f"normed{k}", [P, TILES, D]) for k in range(2)]
        x_hi = [sb(f"x_hi{k}", [P, KD, CHUNK], F16) for k in range(2)]
        x_lo = [sb(f"x_lo{k}", [P, KD, CHUNK], F16) for k in range(2)]
        forget = sb("forget", [P, KD, CHUNK])
        inp = sb("inp", [P, KD, CHUNK])
        cand_sig = sb("cand_sig", [P, KD, CHUNK])
        cand_lin = sb("cand_lin", [P, KD, CHUNK])
        cand = sb("cand", [P, KD, CHUNK])
        value = sb("value", [P, KD, CHUNK])
        hid = sb("hid", [P, KD, CHUNK])
        low = sb("low", [P, CHUNK], F16)
        relu = sb("relu", [P, 2, 2, CHUNK])
        sq = sb("sq", [P, 2, 2, CHUNK])
        sq_hi = sb("sq_hi", [P, FC, CHUNK], F16)
        sq_lo = sb("sq_lo", [P, FC, CHUNK], F16)
        y_sb = sb("y_sb", [P, TILES, D])
        out_sb = sb("out_sb", [P, 2, TILES, D])

        ids_sb = sb("ids_sb", [P, P], I32)
        ids_f = sb("ids_f", [P, 4, P])
        w_raw = sb("w_raw", [P, 6, D])
        w_max = sb("w_max", [P, 6])
        w_pow = sb("w_pow", [P, 6], I32)
        w_inv = sb("w_inv", [P, 6])
        fc_raw = sb("fc_raw", [P, FC, D])
        fc_a = sb("fc_a", [P, FC, D])
        fc_s = sb("fc_s", [P, 3, FC])
        fc_inv = sb("fc_inv", [P, FC])
        pj_raw = sb("pj_raw", [P, KD, HID])
        pj_a = sb("pj_a", [P, KD, HID])
        pj_s = sb("pj_s", [P, 3, KD])
        pj_b = sb("pj_b", [P, KD, P])
        u_raw = sb("u_raw", [P, FC, R])
        u_0 = sb("u_0", [P, FC, R])
        u_1 = sb("u_1", [P, FC, R])
        u_hi = sb("u_hi", [P, FC, R], F16)
        u_parts = sb("u_parts", [P, FC, 2, 2, 2, R])
        u_sum = sb("u_sum", [P, FC])
        u_max = sb("u_max", [P, FC])
        u_pow = sb("u_pow", [P, FC], I32)
        u_inv = sb("u_inv", [P, FC])
        bound = sb("bound", [P, FC])
        bound_1 = sb("bound_1", [P, 1])
        bound_b = sb("bound_b", [P, P])
        bound_2 = sb("bound_2", [P, 1])
        bound_pow = sb("bound_pow", [P, 1], I32)
        shrink = sb("shrink", [P, 1])
        grow = sb("grow", [P, 1])
        gate_sb = sb("gate_sb", [P, 1])
        v_sb = sb("v_sb", [R, D])
        fb_sb = sb("fb_sb", [R, R])
        fb_t = sb("fb_t", [R, R])
        a_sb = sb("a_sb", [R, D])
        a_sq = sb("a_sq", [R, D])
        a_ss = sb("a_ss", [R, 1])
        a_norm = sb("a_norm", [R, 1])
        a_pow = sb("a_pow", [R, 1], I32)
        a_inv = sb("a_inv", [R, 1])
        a_nb = sb("a_nb", [R, P])
        plus_half = sb("plus_half", [R, 1])
        ones = sb("ones", [P, P])
        a_hi = sb("a_hi", [P, KD, R], F16)

        turned = ctx.enter_context(nc.psum_tensor("turned", [P, 1024], F32))
        y_ps = ctx.enter_context(nc.psum_tensor("y_ps", [P, TILES, D], F32))
        bank = [ctx.enter_context(nc.psum_tensor(f"bank{k}", [P, CHUNK], F32)) for k in range(4)]
        turned_cols = turned[:, :].rearrange("p (k t) -> p k t", k=KD)
        turned_rows = turned[:, :].rearrange("p (j d) -> p j d", j=TILES)

        ids_in, w_in, fc_in, pj_in, low_in = (sem(x) for x in ("ids_in", "w_in", "fc_in", "pj_in", "low_in"))
        blank_ready, ident_ready, consts_ready = sem("blank_ready"), sem("ident_ready"), sem("consts_ready")
        dve_chain = sem("dve_chain")
        ids_turned, idx_ready, ids_masked = sem("ids_turned"), sem("idx_ready"), sem("ids_masked")
        w_scaled, w_turned, w_hi_ready, w_lo_ready = (sem(x) for x in ("w_scaled", "w_turned", "w_hi_ready", "w_lo_ready"))
        fb_turned, fb_ready, a_ready, a_summed, a_rooted, a_scaled, a_turned, low_a_ready = (sem(x) for x in (
            "fb_turned", "fb_ready", "a_ready", "a_summed", "a_rooted", "a_scaled", "a_turned", "low_a_ready"))
        anorm_spread, bound_set, bound_spread, u_ready, u_turned, u_copied = (sem(x) for x in (
            "anorm_spread", "bound_set", "bound_spread", "u_ready", "u_turned", "u_copied"))
        fc_ready, fc_turned, fc_copied, pj_ready, pj_turned, pj_copied, pj_spread, weights_ready = (sem(x) for x in (
            "fc_ready", "fc_turned", "fc_copied", "pj_ready", "pj_turned", "pj_copied", "pj_spread", "weights_ready"))

        pool_passed, dve_passed = sem("pool_passed"), sem("dve_passed")
        raw_cleared = sem("raw_cleared")
        idx_set = sem("idx_set")
        gathered = [sem("gathered_even"), sem("gathered_odd")]
        raw_split = sem("raw_split")
        h0_ready = sem("h0_ready")
        stats_ready = [sem("stats_ready0"), sem("stats_ready1")]
        moments_ready = [sem("moments_ready0"), sem("moments_ready1")]
        var_ready = [sem("var_ready0"), sem("var_ready1")]
        rstd_ready = [sem("rstd_ready0"), sem("rstd_ready1")]
        normed_ready = [sem("normed_ready0"), sem("normed_ready1")]
        x_turned = [sem("x_turned0"), sem("x_turned1")]
        x_hi_ready = [sem("x_hi_ready0"), sem("x_hi_ready1")]
        x_lo_ready = [sem("x_lo_ready0"), sem("x_lo_ready1")]
        gate_done = sem("gate_done")
        gate_taken = sem("gate_taken")
        cand_ready = sem("cand_ready")
        value_ready = sem("value_ready")
        scanned = sem("scanned")
        hid_turned = sem("hid_turned")
        h1_ready = sem("h1_ready")
        low_done = sem("low_done")
        low_hi_ready = sem("low_hi_ready")
        low_ready = sem("low_ready")
        fc_done = sem("fc_done")
        relu_ready = sem("relu_ready")
        sq_ready = sem("sq_ready")
        sq_hi_ready = sem("sq_hi_ready")
        sq_lo_ready = sem("sq_lo_ready")
        y_done = sem("y_done")
        y_scaled = sem("y_scaled")
        out_ready = sem("out_ready")
        stored = [sem("stored_even"), sem("stored_odd")]

        def wait(eng, s, count):
            if not isinstance(count, int) or count > 0:
                eng.wait_ge(s, count)

        def pass_on(eng, passed, n):
            if not isinstance(n, int):
                eng.sem_inc(passed, 1)

        def steps(eng, step):
            for n in range(FIRST_LOOP):
                step(n, n // 2, n % 2)
            with eng.Fori(0, (LAST_LOOP + 1 - FIRST_LOOP) // 2) as i:
                step(i * 2 + FIRST_LOOP, i + FIRST_LOOP // 2, FIRST_LOOP % 2)
                step(i * 2 + FIRST_LOOP + 1, i + (FIRST_LOOP + 1) // 2, (FIRST_LOOP + 1) % 2)
            for n in range(LAST_LOOP + 1, N + 1):
                step(n, n // 2, n % 2)

        def known_below(n, limit):
            return not isinstance(n, int) or n < limit

        block = ctx.enter_context(nc.Block())

        @block.sync
        def _(sp):
            sp.dma_start(ids_sb[:, :], ids.rearrange("b (h p) -> (b h) p", p=P)).then_inc(ids_in, 16)
            for g, w in enumerate((wf, wi, wh)):
                sp.dma_start(w_raw[:, 2 * g:2 * g + 2, :], w.rearrange("(h p) d -> p h d", p=P)).then_inc(w_in, 16)
            sp.dma_start(v_sb[:, :], v[:, :]).then_inc(low_in, 16)
            sp.dma_start(fb_sb[:, :], fast_b[:, :]).then_inc(low_in, 16)
            sp.dma_start(gate_sb[:, :], gate.partition_broadcast(P)).then_inc(low_in, 16)
            sp.dma_start(u_raw[:, :, :], u.rearrange("(g p) r -> p g r", p=P)).then_inc(low_in, 16)
            sp.dma_start(fc_raw[:, :, :], w_fc.rearrange("(g p) d -> p g d", p=P)).then_inc(fc_in, 16)
            sp.dma_start(pj_raw[:, :, :], w_proj.rearrange("(g p) f -> p g f", p=P)).then_inc(pj_in, 16)

            def step(n, h, par):
                if isinstance(n, int) and n == 0:
                    return
                m, even = n - 1, 1 - par
                first = sp.snap(m * CHUNK) if not isinstance(m, int) else m * CHUNK
                sp.wait_ge(out_ready, m + 1)
                sp.dma_start(out[bass.ds(first, CHUNK), :].rearrange("(j p) d -> p j d", p=P),
                             out_sb[:, even, :, :]).then_inc(stored[even], 16)

            steps(sp, step)
            for s in stored:
                sp.wait_ge(s, 16 * (N // 2))

        @block.gpsimd
        def _(pool):
            pool.memset(ident[:, :], 0.0).then_inc(blank_ready, 1)
            pool.memset(minus_half[:, :], -0.5).then_inc(consts_ready, 1)
            pool.memset(plus_half[:, :], 0.5).then_inc(consts_ready, 1)
            pool.memset(ones[:, :], 1.0).then_inc(consts_ready, 1)
            pool.wait_ge(blank_ready, 1)
            pool.affine_select(out=ident[:, :], in_=ident[:, :], compare_op=ALU.not_equal, fill=1.0, base=0,
                               pattern=[[-1, P]], channel_multiplier=1).then_inc(ident_ready, 1)

            def gather(c, h, par):
                wait(pool, raw_split, 2 * (c - 1))
                pass_on(pool, pool_passed, c)
                pool.memset(rows_raw[:, par, :, :], 0.0).then_inc(raw_cleared, 1)
                pool.tensor_copy(idx_now[:, par, :], idx_all[:, bass.ds(c * TILES, TILES)]).then_inc(idx_set, 1)
                pool.wait_ge(raw_cleared, c + 1)
                pool.wait_ge(idx_set, c + 1)
                pass_on(pool, pool_passed, c)
                for j in range(TILES):
                    pool.indirect_dma_start(
                        rows_raw[:, par, j, :], None, table,
                        bass.IndirectOffsetOnAxis(ap=idx_now[:, par, j:j + 1], axis=0),
                        bounds_check=V - 1, oob_is_err=False).then_inc(gathered[par], 16)

            def root(k, c):
                pool.wait_ge(moments_ready[k], TILES * (c + 1))
                pass_on(pool, pool_passed, c)
                pool.tensor_scalar(var_eps[k][:, :], moments[k][:, :, 1], EPS, None, ALU.add)\
                    .then_inc(var_ready[k], 1)
                pool.wait_ge(var_ready[k], c + 1)
                pool.tensor_tensor(rstd[k][:, :], var_eps[k][:, :], minus_half[:, :], ALU.pow)\
                    .then_inc(rstd_ready[k], 1)

            pool.wait_ge(idx_ready, 1)
            pool.wait_ge(consts_ready, 3)
            gather(0, 0, 0)
            gather(1, 0, 1)
            root(0, 0)
            pool.wait_ge(a_summed, 1)
            pool.tensor_tensor(a_norm[:, :], a_ss[:, :], plus_half[:, :], ALU.pow).then_inc(a_rooted, 1)
            gather(2, 1, 0)

            def step(n, h, par):
                m = n - 1
                if known_below(n, N - 3):
                    gather(n + 3, None, 1 - par)
                if known_below(n, N - 1):
                    root(0, n + 1)
                if known_below(n, N):
                    for e in range(KD):
                        pool.wait_ge(cand_ready, 2 * n + e + 1)
                        wait(pool, scanned, 4 * (n - 1) + 2 * e + 2)
                        pool.wait_ge(gate_taken, 8 * n + 4 * e + 4)
                        pool.tensor_tensor(value[:, e, :], inp[:, e, :], cand[:, e, :], ALU.mult)\
                            .then_inc(value_ready, 1)
                    root(1, n)
                if not isinstance(n, int) or n > 0:
                    wait(pool, stored[1 - par], (h if par else h - 1) * 16)
                    pool.wait_ge(h1_ready, m + 1)
                    pool.wait_ge(y_scaled, m + 1)
                    pool.tensor_tensor(out_sb[:, 1 - par, :, :], y_sb[:, :, :], h1[:, 1 - par, :, :], ALU.add)\
                        .then_inc(out_ready, 1)

            steps(pool, step)

        @block.scalar
        def _(act):
            for b in range(3):
                act.wait_ge(w_turned, b + 1)
                act.activation(w_hi[:, :, :, :].rearrange("p k g e -> p (k g e)")[:, b * 512:(b + 1) * 512],
                               bank[b][:, :], ACT.Copy).then_inc(w_hi_ready, 1)

            def x_high(k, c):
                act.wait_ge(x_turned[k], c + 1)
                act.activation(x_hi[k][:, :, :], turned_cols, ACT.Copy).then_inc(x_hi_ready[k], 1)

            x_high(0, 0)

            def step(n, h, par):
                m = n - 1
                front = known_below(n, N)
                back = not isinstance(n, int) or n > 0
                if back:
                    wait(act, fc_done, FC * m)
                    x_high(1, m)
                if front:
                    for e in range(KD):
                        for q, (dst, func, bias) in enumerate((
                                (forget, ACT.Sigmoid, 0.0), (inp, ACT.Sigmoid, 0.0),
                                (cand_sig, ACT.Sigmoid, 0.0), (cand_lin, ACT.Identity, 0.5))):
                            g = min(q, 2)
                            act.wait_ge(gate_done, 6 * n + 3 * e + g + 1)
                            if q == 0:
                                wait(act, scanned, 4 * (n - 1) + 2 * e + 2)
                            if q == 1:
                                wait(act, value_ready, 2 * (n - 1) + e + 1)
                            if q >= 2:
                                wait(act, cand_ready, 2 * (n - 1) + e + 1)
                            act.activation(dst[:, e, :], bank[(3 * e + g) % 4][:, :], func, bias=bias,
                                           scale=w_back[:, 2 * g + e:2 * g + e + 1]).then_inc(gate_taken, 1)
                if back:
                    act.wait_ge(low_done, m + 1)
                    wait(act, fc_done, FC * m)
                    act.activation(low[:, :], bank[2][:, :], ACT.Copy).then_inc(low_hi_ready, 1)
                for p in range(FC // 2):
                    if back:
                        for f in (2 * p, 2 * p + 1):
                            act.wait_ge(fc_done, FC * m + f + 1)
                            wait(act, sq_ready, 4 * m + p - 1)
                            act.activation(relu[:, p % 2, f % 2, :], bank[(7 + f) % 4][:, :], ACT.Relu,
                                           scale=relu_scale[:, f:f + 1]).then_inc(relu_ready, 1)
                        act.wait_ge(relu_ready, FC * m + 2 * p + 2)
                        wait(act, sq_lo_ready, 4 * m + p - 1)
                        act.activation(sq[:, p % 2, :, :], relu[:, p % 2, :, :], ACT.Square)\
                            .then_inc(sq_ready, 1)
                    if p == 1 and known_below(n, N - 1):
                        act.wait_ge(gate_done, 6 * (n + 1))
                        x_high(0, n + 1)

            steps(act, step)

        @block.tensor
        def _(pe):
            pe.wait_ge(ident_ready, 1)
            pe.wait_ge(ids_masked, 1)
            pe.transpose(y_ps[:, 0, 0:P], ids_f[:, 3, :], ident[:, :]).then_inc(ids_turned, 1)
            pe.wait_ge(w_scaled, 1)
            for b in range(3):
                for q in range(4):
                    k, g = divmod(4 * b + q, 6)
                    ins = pe.transpose(bank[b][:, q * P:(q + 1) * P], w_raw[:, g, k * P:(k + 1) * P], ident[:, :])
                ins.then_inc(w_turned, 1)
            pe.wait_ge(low_in, 64)
            pe.transpose(bank[3][0:R, 0:R], fb_sb[:, :], ident[0:R, 0:R]).then_inc(fb_turned, 1)
            pe.wait_ge(fb_ready, 1)
            pe.matmul(y_ps[0:R, 1, :], fb_t[:, :], v_sb[:, :], start=True, stop=True).then_inc(a_ready, 1)
            pe.wait_ge(a_scaled, 2)
            for k in range(KD):
                pe.transpose(bank[3][:, 128 + k * R:128 + (k + 1) * R], a_sb[:, k * P:(k + 1) * P], ident[0:R, 0:R])\
                    .then_inc(a_turned, 1)
            pe.matmul(y_ps[:, 2, 0:R], a_nb[:, :], ident[0:R, 0:R], start=True, stop=True).then_inc(anorm_spread, 1)

            def turn(k, c):
                pe.wait_ge(normed_ready[k], TILES * (c + 1))
                for e in range(KD):
                    for j in range(TILES):
                        ins = pe.transpose(turned_cols[:, e, j * P:(j + 1) * P],
                                           normed[k][:, j, e * P:(e + 1) * P], ident[:, :])
                ins.then_inc(x_turned[k], 1)

            turn(0, 0)
            pe.wait_ge(bound_set, 1)
            pe.transpose(y_ps[:, 3, 0:P], bound_b[:, :], ident[:, :]).then_inc(bound_spread, 1)

            pe.wait_ge(fc_ready, FC)
            for b in range(4):
                if b < 3:
                    pe.wait_ge(w_lo_ready, b + 1)
                else:
                    pe.wait_ge(low_a_ready, 1)
                for q in range(4):
                    k, g = divmod(4 * b + q, FC)
                    ins = pe.transpose(bank[b][:, q * P:(q + 1) * P], fc_raw[:, g, k * P:(k + 1) * P], ident[:, :])
                ins.then_inc(fc_turned, 1)
            pe.wait_ge(u_ready, 1)
            for b in range(2):
                pe.wait_ge(fc_copied, b + 1)
                for q in range(4):
                    ins = pe.transpose(bank[b][:, q * P:(q + 1) * P],
                                       u_parts[:, 4 * b + q, :, :, :, :].rearrange("p a b c r -> p (a b c r)"),
                                       ident[:, :])
                ins.then_inc(u_turned, 1)
            pe.wait_ge(pj_ready, KD)
            for b in range(4):
                if b < 2:
                    pe.wait_ge(fc_copied, b + 3)
                else:
                    pe.wait_ge(u_copied, b - 1)
                for q in range(4):
                    f, k = divmod(4 * b + q, KD)
                    ins = pe.transpose(bank[(b + 2) % 4][:, q * P:(q + 1) * P],
                                       pj_raw[:, k, f * P:(f + 1) * P], ident[:, :])
                ins.then_inc(pj_turned, 1)
            for k in range(KD):
                ins = pe.matmul(y_ps[:, 0, k * P:(k + 1) * P], pj_b[:, k, :], ident[:, :], start=True, stop=True)
            ins.then_inc(pj_spread, 1)
            pe.wait_ge(weights_ready, 1)

            def step(n, h, par):
                m = n - 1
                front = known_below(n, N)
                back = not isinstance(n, int) or n > 0
                if front:
                    pe.wait_ge(x_hi_ready[0], n + 1)
                    pe.wait_ge(x_lo_ready[0], n + 1)
                    for p in range(6):
                        e, g = divmod(p, 3)
                        if p < 4:
                            wait(pe, relu_ready, FC * (n - 2) + (6, 7, 8, 5)[p])
                            if isinstance(n, int) and n == 1:
                                pe.wait_ge(gate_taken, 8)
                        else:
                            pe.wait_ge(gate_taken, 8 * n + p - 3)
                        q = 2 * g + e
                        for k in range(KD):
                            for w in (w_hi, w_lo):
                                for x in (x_hi, x_lo):
                                    ins = pe.matmul(bank[p % 4][:, :], w[:, k, q, :], x[0][:, k, :],
                                                    start=(k == 0 and w is w_hi and x is x_hi),
                                                    stop=(k == KD - 1 and w is w_lo and x is x_lo))
                        ins.then_inc(gate_done, 1)
                if back:
                    pe.wait_ge(x_hi_ready[1], m + 1)
                    pe.wait_ge(x_lo_ready[1], m + 1)
                    if front:
                        pe.wait_ge(gate_taken, 8 * n + 4)
                    else:
                        pe.wait_ge(relu_ready, FC * (n - 2) + 8)
                    for k in range(KD):
                        pe.matmul(bank[2][:, :], low_a[:, k, :], x_hi[1][:, k, :], start=(k == 0), stop=False)
                        ins = pe.matmul(bank[2][:, :], low_a[:, k, :], x_lo[1][:, k, :], start=False, stop=(k == KD - 1))
                    ins.then_inc(low_done, 1)
                for f in range(FC):
                    if back:
                        if f < 3 and front:
                            pe.wait_ge(gate_taken, 8 * n + (5, 6, 8)[f])
                        elif f < 3:
                            pe.wait_ge(relu_ready, FC * (n - 2) + 5 + f)
                        elif f > 3:
                            pe.wait_ge(relu_ready, FC * m + f - 3)
                        else:
                            pe.wait_ge(low_ready, m + 1)
                        dst = bank[(7 + f) % 4]
                        for k in range(KD):
                            pe.matmul(dst[:, :], fc_t[:, k, f * P:(f + 1) * P], x_hi[1][:, k, :],
                                      start=(k == 0), stop=False)
                            pe.matmul(dst[:, :], fc_t[:, k, f * P:(f + 1) * P], x_lo[1][:, k, :],
                                      start=False, stop=False)
                        if f == 0:
                            pe.wait_ge(low_ready, m + 1)
                        pe.matmul(dst[:, :], low_u[:, f * P:(f + 1) * P], low[:, :], start=False, stop=True)\
                            .then_inc(fc_done, 1)
                    if f == 3 and known_below(n, N - 1):
                        wait(pe, x_hi_ready[1], n)
                        wait(pe, x_lo_ready[1], n)
                        turn(0, n + 1)
                if front:
                    pe.wait_ge(scanned, 4 * (n + 1))
                    ahead = min(n + 2, N) if isinstance(n, int) else n + 2
                    pe.wait_ge(x_hi_ready[0], ahead)
                    pe.wait_ge(x_lo_ready[0], ahead)
                    for j in range(TILES):
                        for e in range(KD):
                            ins = pe.transpose(turned_rows[:, j, e * P:(e + 1) * P],
                                               hid[:, e, j * P:(j + 1) * P], ident[:, :])
                    ins.then_inc(hid_turned, 1)
                if back:
                    wait(pe, y_scaled, m)
                    for f in range(FC):
                        if f % 2 == 0:
                            pe.wait_ge(sq_hi_ready, 4 * m + f // 2 + 1)
                            pe.wait_ge(sq_lo_ready, 4 * m + f // 2 + 1)
                        for j in range(TILES):
                            for part in (sq_hi, sq_lo):
                                ins = pe.matmul(y_ps[:, j, :], part[:, f, j * P:(j + 1) * P], proj_t[:, f, :],
                                                start=(f == 0 and j % 2 == 0 and part is sq_hi),
                                                stop=(f == FC - 1 and part is sq_lo), skip_group_check=True)
                    ins.then_inc(y_done, 1)
                if front:
                    pe.wait_ge(h1_ready, n + 1)
                    turn(1, n)

            steps(pe, step)

        @block.vector
        def _(dve):
            chain = [0]

            def mark(ins):
                chain[0] += 1
                return ins.then_inc(dve_chain, 1)

            def settle():
                dve.wait_ge(dve_chain, chain[0])

            dve.wait_ge(ids_in, 16)
            mark(dve.tensor_copy(ids_f[:, 0, :], ids_sb[:, :]))
            settle()
            mark(dve.tensor_scalar(ids_f[:, 1, :], ids_f[:, 0, :], 0.0, float(V), ALU.is_lt, ALU.mult))
            settle()
            mark(dve.tensor_tensor(ids_f[:, 0, :], ids_f[:, 0, :], ids_f[:, 1, :], ALU.add))
            settle()
            mark(dve.tensor_scalar(ids_f[:, 1, :], ids_f[:, 0, :], 0.0, None, ALU.is_ge))
            settle()
            mark(dve.scalar_tensor_tensor(ids_f[:, 2, :], ids_f[:, 0, :], float(V), ids_f[:, 1, :], ALU.is_lt, ALU.mult))
            settle()
            mark(dve.scalar_tensor_tensor(ids_f[:, 1, :], ids_f[:, 0, :], -float(V), ids_f[:, 2, :], ALU.add, ALU.mult))
            settle()
            dve.tensor_scalar(ids_f[:, 3, :], ids_f[:, 1, :], float(V), None, ALU.add).then_inc(ids_masked, 1)
            dve.wait_ge(ids_turned, 1)
            dve.tensor_copy(idx_all[:, :], y_ps[:, 0, 0:P]).then_inc(idx_ready, 1)

            dve.wait_ge(w_in, 48)
            mark(dve.tensor_reduce(w_max[:, :], w_raw[:, :, :], AX, ALU.max, apply_absolute_value=True))
            settle()
            mark(dve.tensor_scalar(w_max[:, :], w_max[:, :], 2.0 ** -60, None, ALU.max))
            settle()
            mark(dve.tensor_scalar(w_pow[:, :], w_max[:, :].bitcast(I32), EXPONENT, None, ALU.bitwise_and))
            settle()
            mark(dve.tensor_scalar(w_back[:, :], w_pow[:, :].bitcast(F32), 1 / W_TOP, None, ALU.mult))
            settle()
            mark(dve.reciprocal(w_inv[:, :], w_back[:, :]))
            settle()
            for g in range(6):
                ins = mark(dve.tensor_scalar(w_raw[:, g, :], w_raw[:, g, :], w_inv[:, g:g + 1], None, ALU.mult))
            settle()
            dve.tensor_copy(w_max[:, 0:1], w_inv[:, 0:1]).then_inc(w_scaled, 1)

            dve.wait_ge(fb_turned, 1)
            dve.tensor_copy(fb_t[:, :], bank[3][0:R, 0:R]).then_inc(fb_ready, 1)
            dve.wait_ge(a_ready, 1)
            mark(dve.tensor_copy(a_sb[:, :], y_ps[0:R, 1, :]))
            settle()
            mark(dve.tensor_tensor(a_sq[:, :], a_sb[:, :], a_sb[:, :], ALU.mult))
            settle()
            dve.tensor_reduce(a_ss[:, :], a_sq[:, :], AX, ALU.add).then_inc(a_summed, 1)

            for b in range(3):
                dve.wait_ge(w_hi_ready, b + 1)
                whole = [w[:, :, :, :].rearrange("p k g e -> p (k g e)")[:, b * 512:(b + 1) * 512] for w in (w_hi, w_lo)]
                dve.tensor_tensor(whole[1], bank[b][:, :], whole[0], ALU.subtract).then_inc(w_lo_ready, 1)

            def guard(c, wait_h, par):
                dve.wait_ge(gathered[par], wait_h)
                wait(dve, h0_ready, c)
                dve.tensor_scalar(rows_pos[:, :, :], rows_raw[:, par, :, :], 0.0, FMAX, ALU.max, ALU.min)\
                    .then_inc(raw_split, 1)
                dve.tensor_scalar(rows_neg[:, :, :], rows_raw[:, par, :, :], 0.0, -FMAX, ALU.min, ALU.max)\
                    .then_inc(raw_split, 1)

            def guard_sum(c, par):
                dve.wait_ge(raw_split, 2 * (c + 1))
                dve.tensor_tensor(h0[:, par, :, :], rows_pos[:, :, :], rows_neg[:, :, :], ALU.add).then_inc(h0_ready, 1)

            def measure(k, c, rows):
                for j in range(TILES):
                    dve.bn_stats(stats[k][:, j, :], rows[:, j, :]).then_inc(stats_ready[k], 1)
                dve.wait_ge(stats_ready[k], TILES * (c + 1))
                pass_on(dve, dve_passed, c)
                for j in range(TILES):
                    dve.bn_aggr(moments[k][:, j, :], stats[k][:, j, :]).then_inc(moments_ready[k], 1)

            def normalise(k, c, rows):
                dve.wait_ge(rstd_ready[k], c + 1)
                wait(dve, x_turned[k], c)
                for j in range(TILES):
                    dve.tensor_scalar(normed[k][:, j, :], rows[:, j, :], moments[k][:, j, 0:1],
                                      rstd[k][:, j:j + 1], ALU.subtract, ALU.mult).then_inc(normed_ready[k], 1)

            def x_low(k, c):
                dve.wait_ge(x_hi_ready[k], c + 1)
                dve.tensor_tensor(x_lo[k][:, :, :], turned_cols, x_hi[k][:, :, :], ALU.subtract)\
                    .then_inc(x_lo_ready[k], 1)

            guard(0, 64, 0)
            guard_sum(0, 0)
            dve.wait_ge(h0_ready, 1)
            measure(0, 0, h0[:, 0, :, :])

            dve.wait_ge(a_rooted, 1)
            mark(dve.tensor_scalar(a_norm[:, :], a_norm[:, :], 2.0 ** -60, None, ALU.max))
            settle()
            mark(dve.tensor_scalar(a_pow[:, :], a_norm[:, :].bitcast(I32), EXPONENT, None, ALU.bitwise_and))
            settle()
            mark(dve.reciprocal(a_inv[:, :], a_pow[:, :].bitcast(F32)))
            settle()
            dve.wait_ge(consts_ready, 3)
            dve.tensor_scalar(a_sb[:, :], a_sb[:, :], a_inv[:, :], LOW_TOP, ALU.mult, ALU.mult).then_inc(a_scaled, 1)
            dve.tensor_scalar(a_nb[:, :], ones[0:R, :], a_pow[:, :].bitcast(F32), None, ALU.mult).then_inc(a_scaled, 1)
            dve.wait_ge(a_turned, KD)
            a_cols = bank[3][:, 128:128 + KD * R].rearrange("p (k r) -> p k r", k=KD)
            mark(dve.tensor_copy(a_hi[:, :, :], a_cols))
            settle()
            low_av = low_a[:, :, :].rearrange("p k (s a u r) -> p k s a u r", s=2, a=2, u=2)
            for s in range(2):
                for q in range(2):
                    mark(dve.tensor_copy(low_av[:, :, s, 0, q, :], a_hi[:, :, :]))
                    ins = dve.tensor_tensor(low_av[:, :, s, 1, q, :], a_cols, a_hi[:, :, :], ALU.subtract)
                    if s * q == 0:
                        mark(ins)
            settle()
            ins.then_inc(low_a_ready, 1)

            normalise(0, 0, h0[:, 0, :, :])
            x_low(0, 0)
            guard(1, 64, 1)
            guard_sum(1, 1)

            dve.wait_ge(fc_in, 16)
            mark(dve.tensor_reduce(fc_s[:, 0, :], fc_raw[:, :, :], AX, ALU.add, apply_absolute_value=True))
            dve.wait_ge(pj_in, 16)
            mark(dve.tensor_reduce(pj_s[:, 0, :], pj_raw[:, :, :], AX, ALU.add, apply_absolute_value=True))
            settle()
            mark(dve.tensor_scalar(fc_s[:, 0, :], fc_s[:, 0, :], 1 / D, 1e-5, ALU.mult, ALU.max))
            mark(dve.tensor_scalar(pj_s[:, 0, :], pj_s[:, 0, :], 1 / HID, 1e-5, ALU.mult, ALU.max))
            settle()
            for q, half in ((1, 0.5), (2, -0.5)):
                mark(dve.tensor_scalar(fc_s[:, q, :], fc_s[:, 0, :], half, None, ALU.mult))
                mark(dve.tensor_scalar(pj_s[:, q, :], pj_s[:, 0, :], half, None, ALU.mult))
            mark(dve.reciprocal(fc_inv[:, :], fc_s[:, 0, :]))

            dve.wait_ge(anorm_spread, 1)
            dve.wait_ge(low_in, 64)
            for g in range(FC):
                mark(dve.scalar_tensor_tensor(u_0[:, g, :], u_raw[:, g, :], gate_sb[:, :], y_ps[:, 2, 0:R],
                                              ALU.mult, ALU.mult))
            settle()
            mark(dve.tensor_reduce(u_sum[:, :], u_0[:, :, :], AX, ALU.add, apply_absolute_value=True))
            settle()
            mark(dve.tensor_scalar(bound[:, :], u_sum[:, :], 32.0, None, ALU.mult))
            settle()
            mark(dve.scalar_tensor_tensor(bound[:, :], fc_s[:, 0, :], 256.0, bound[:, :], ALU.mult, ALU.add))
            settle()
            mark(dve.tensor_reduce(bound_1[:, :], bound[:, :], AX, ALU.max))
            settle()
            dve.tensor_scalar(bound_b[:, :], ones[:, :], bound_1[:, :], None, ALU.mult).then_inc(bound_set, 1)
            for g in range(FC):
                mark(dve.tensor_scalar(u_1[:, g, :], u_0[:, g, :], fc_inv[:, g:g + 1], 1 / LOW_TOP, ALU.mult, ALU.mult))
            settle()
            mark(dve.tensor_reduce(u_max[:, :], u_1[:, :, :], AX, ALU.max, apply_absolute_value=True))
            settle()
            mark(dve.tensor_scalar(u_max[:, :], u_max[:, :], 2.0 ** -10, None, ALU.max))
            settle()
            mark(dve.tensor_scalar(u_pow[:, :], u_max[:, :].bitcast(I32), EXPONENT, None, ALU.bitwise_and))
            settle()
            mark(dve.tensor_scalar(u_max[:, :], u_pow[:, :].bitcast(F32), 1 / LOW_TOP, None, ALU.mult))
            settle()
            mark(dve.reciprocal(u_inv[:, :], u_max[:, :]))
            settle()
            for g in range(FC):
                mark(dve.tensor_scalar(u_1[:, g, :], u_1[:, g, :], u_inv[:, g:g + 1], None, ALU.mult))
            settle()
            mark(dve.tensor_copy(u_hi[:, :, :], u_1[:, :, :]))
            settle()
            mark(dve.tensor_copy(u_0[:, :, :], u_hi[:, :, :]))
            settle()
            mark(dve.tensor_tensor(u_1[:, :, :], u_1[:, :, :], u_0[:, :, :], ALU.subtract))
            settle()
            for s in range(2):
                for a in range(2):
                    mark(dve.tensor_copy(u_parts[:, :, s, a, 0, :], u_0[:, :, :]))
                    mark(dve.tensor_copy(u_parts[:, :, s, a, 1, :], u_1[:, :, :]))
            settle()
            dve.wait_ge(bound_spread, 1)
            mark(dve.tensor_reduce(bound_2[:, :], y_ps[:, 3, 0:P], AX, ALU.max))
            settle()
            mark(dve.tensor_scalar(bound_pow[:, :], bound_2[:, :].bitcast(I32), EXPONENT, None, ALU.bitwise_and))
            settle()
            mark(dve.tensor_scalar(grow[:, :], bound_pow[:, :].bitcast(F32), 1 / RELU_TOP, None, ALU.mult))
            settle()
            mark(dve.reciprocal(shrink[:, :], grow[:, :]))
            mark(dve.tensor_tensor(relu_scale[:, :], fc_s[:, 0, :], u_max[:, :], ALU.mult))
            settle()
            mark(dve.tensor_scalar(relu_scale[:, :], relu_scale[:, :], shrink[:, :], None, ALU.mult))
            mark(dve.tensor_tensor(grow[:, :], grow[:, :], grow[:, :], ALU.mult))
            settle()
            dve.tensor_copy(bound_1[:, :], grow[:, :]).then_inc(u_ready, 1)

            for g in range(FC):
                mark(dve.tensor_scalar(fc_a[:, g, :], fc_raw[:, g, :], fc_s[:, 2, g:g + 1], None, ALU.is_lt))
                settle()
                mark(dve.scalar_tensor_tensor(fc_raw[:, g, :], fc_raw[:, g, :], fc_s[:, 1, g:g + 1], fc_a[:, g, :],
                                              ALU.is_gt, ALU.subtract))
                settle()
                dve.tensor_scalar(fc_raw[:, g, :], fc_raw[:, g, :], u_inv[:, g:g + 1], None, ALU.mult)\
                    .then_inc(fc_ready, 1)
            for b in range(4):
                k, g = divmod(4 * b, FC)
                dve.wait_ge(fc_turned, b + 1)
                dve.tensor_copy(fc_t[:, k, g * P:(g + 4) * P], bank[b][:, :]).then_inc(fc_copied, 1)
            for b in range(2):
                dve.wait_ge(u_turned, b + 1)
                dve.tensor_copy(low_u[:, b * 512:(b + 1) * 512], bank[b][:, :]).then_inc(u_copied, 1)
            for k in range(KD):
                mark(dve.tensor_scalar(pj_a[:, k, :], pj_raw[:, k, :], pj_s[:, 2, k:k + 1], None, ALU.is_lt))
                mark(dve.tensor_scalar(pj_b[:, k, :], ones[:, :], pj_s[:, 0, k:k + 1], None, ALU.mult))
                settle()
                dve.scalar_tensor_tensor(pj_raw[:, k, :], pj_raw[:, k, :], pj_s[:, 1, k:k + 1], pj_a[:, k, :],
                                         ALU.is_gt, ALU.subtract).then_inc(pj_ready, 1)
            for b in range(4):
                dve.wait_ge(pj_turned, b + 1)
                mark(dve.tensor_copy(proj_t[:, 2 * b:2 * b + 2, :],
                                     bank[(b + 2) % 4][:, :].rearrange("p (f d) -> p f d", f=2)))
            dve.wait_ge(pj_spread, 1)
            mark(dve.tensor_scalar(proj_scale[:, :], y_ps[:, 0, :], grow[:, :], None, ALU.mult))
            settle()
            dve.tensor_copy(bound_1[:, :], grow[:, :]).then_inc(weights_ready, 1)

            def step(n, h, par):
                m = n - 1
                front = known_below(n, N)
                back = not isinstance(n, int) or n > 0
                if back:
                    wait(dve, fc_done, FC * m)
                    x_low(1, m)
                if known_below(n, N - 1):
                    dve.wait_ge(h0_ready, n + 2)
                    measure(0, n + 1, h0[:, 1 - par, :, :])

                def candidate(e):
                    dve.wait_ge(gate_taken, 8 * n + 4 * e + 4)
                    wait(dve, value_ready, 2 * (n - 1) + e + 1)
                    dve.tensor_tensor(cand[:, e, :], cand_lin[:, e, :], cand_sig[:, e, :], ALU.max)\
                        .then_inc(cand_ready, 1)

                def scan(e):
                    dve.wait_ge(value_ready, 2 * n + e + 1)
                    wait(dve, hid_turned, n)
                    for s in range(CHUNK // T):
                        at = slice(s * T, (s + 1) * T)
                        dve.tensor_tensor_scan(hid[:, e, at], forget[:, e, at], value[:, e, at], 0.5,
                                               ALU.mult, ALU.add).then_inc(scanned, 1)

                if front:
                    candidate(0)
                if known_below(n, N - 1):
                    normalise(0, n + 1, h0[:, 1 - par, :, :])
                if front:
                    scan(0)
                    candidate(1)
                if back:
                    dve.wait_ge(low_hi_ready, m + 1)
                    dve.tensor_tensor(low[64:P, :], bank[2][64:P, :], low[64:P, :], ALU.subtract)\
                        .then_inc(low_ready, 1)
                if front:
                    scan(1)
                for p in range(FC // 2):
                    if back:
                        dve.wait_ge(sq_ready, 4 * m + p + 1)
                        wait(dve, y_done, m)
                        dve.tensor_copy(sq_hi[:, 2 * p:2 * p + 2, :], sq[:, p % 2, :, :]).then_inc(sq_hi_ready, 1)
                        dve.wait_ge(sq_hi_ready, 4 * m + p + 1)
                        dve.tensor_tensor(sq_lo[:, 2 * p:2 * p + 2, :], sq[:, p % 2, :, :],
                                          sq_hi[:, 2 * p:2 * p + 2, :], ALU.subtract).then_inc(sq_lo_ready, 1)
                    if p == 1 and known_below(n, N - 1):
                        dve.wait_ge(gate_done, 6 * (n + 1))
                        x_low(0, n + 1)
                if front:
                    dve.wait_ge(hid_turned, n + 1)
                    wait(dve, out_ready, n - 1)
                    dve.tensor_tensor(h1[:, par, :, :], turned_rows, h0[:, par, :, :], ALU.add).then_inc(h1_ready, 1)
                    dve.wait_ge(h1_ready, n + 1)
                    measure(1, n, h1[:, par, :, :])
                if known_below(n, N - 2):
                    guard(n + 2, 64 * (h + 2), par)
                if front:
                    normalise(1, n, h1[:, par, :, :])
                if known_below(n, N - 2):
                    guard_sum(n + 2, par)
                if back:
                    dve.wait_ge(y_done, m + 1)
                    wait(dve, out_ready, m)
                    dve.tensor_tensor(y_sb[:, :, :], y_ps[:, :, :],
                                      proj_scale[:, :].unsqueeze(1).to_broadcast([P, TILES, D]), ALU.mult)\
                        .then_inc(y_scaled, 1)

            steps(dve, step)


def kernel(x, L0_tok_embed_table, L0_attn_Wf, L0_attn_Wi, L0_attn_Wh, L0_ffn_fast_b, L0_ffn_w_fc, L0_ffn_w_proj,
           L0_ffn_u, L0_ffn_v, L0_ffn_gate):
    import numpy as np
    import concourse.bacc as bacc
    from concourse.bass_utils import run_bass_kernel_spmd

    nc = bacc.Bacc("TRN2", target_bir_lowering=False, num_devices=1)
    given = {
        "ids": x, "table": L0_tok_embed_table, "wf": L0_attn_Wf, "wi": L0_attn_Wi, "wh": L0_attn_Wh,
        "fast_b": L0_ffn_fast_b, "w_fc": L0_ffn_w_fc, "w_proj": L0_ffn_w_proj, "u": L0_ffn_u, "v": L0_ffn_v,
        "gate": np.asarray(L0_ffn_gate).reshape(1, 1),
    }
    arrays = {name: np.ascontiguousarray(a) for name, a in given.items()}
    aps = [nc.dram_tensor(name, a.shape, mybir.dt.from_np(a.dtype), kind="ExternalInput").ap()
           for name, a in arrays.items()]
    out = nc.dram_tensor("out", (SEQS * T, D), F32, kind="ExternalOutput").ap()
    build(nc, *aps, out)
    result = run_bass_kernel_spmd(nc, [arrays], core_ids=[0])
    return result.results[0]["out"].reshape(SEQS, T, D)
```

```python
from contextlib import ExitStack

import concourse.bass as bass
from concourse import mybir

ALU = mybir.AluOpType
ACT = mybir.ActivationFunctionType
AX = mybir.AxisListType.X
F32 = mybir.dt.float32
F16 = mybir.dt.float16
BF16 = mybir.dt.bfloat16
I32 = mybir.dt.int32

P = 128
SEQS, T = 64, 256
D = 256
V = 32768
HID = 1024
R = 16
CHUNK = 512
N = SEQS * T // CHUNK
TILES = CHUNK // P
KD = D // P
FC = HID // P
EPS = 1e-5
FMAX = 3.4028234663852886e38
EXPONENT = 0x7F800000
W_TOP = 2.0 ** 10
LOW_TOP = 2.0 ** 10
RELU_TOP = 2.0 ** 6

FIRST_LOOP, LAST_LOOP = 3, N - 4


def build(nc, ids, table, wf, wi, wh, fast_b, w_fc, w_proj, u, v, gate, out):
    ctx = ExitStack()
    with ctx:
        def sb(name, shape, dt=F32):
            return ctx.enter_context(nc.sbuf_tensor(name, shape, dt))

        def sem(name):
            return ctx.enter_context(nc.semaphore(name))

        ident = sb("ident", [P, P])
        w_hi = sb("w_hi", [P, KD, 6, P], F16)
        w_lo = sb("w_lo", [P, KD, 6, P], F16)
        w_back = sb("w_back", [P, 6])
        fc_t = sb("fc_t", [P, KD, HID], BF16)
        low_a = sb("low_a", [P, KD, P], F16)
        low_u = sb("low_u", [P, HID], F16)
        relu_scale = sb("relu_scale", [P, FC])
        proj_t = sb("proj_t", [P, FC, D], BF16)
        proj_scale = sb("proj_scale", [P, D])
        minus_half = sb("minus_half", [P, TILES])
        idx_all = sb("idx_all", [P, N * TILES], I32)

        idx_now = sb("idx_now", [P, 2, TILES], I32)
        rows_raw = sb("rows_raw", [P, 2, TILES, D])
        rows_pos = sb("rows_pos", [P, TILES, D])
        rows_neg = sb("rows_neg", [P, TILES, D])
        h0 = sb("h0", [P, 2, TILES, D])
        h1 = sb("h1", [P, 2, TILES, D])
        stats = [sb(f"stats{k}", [P, TILES, 6]) for k in range(2)]
        moments = [sb(f"moments{k}", [P, TILES, 2]) for k in range(2)]
        var_eps = [sb(f"var_eps{k}", [P, TILES]) for k in range(2)]
        rstd = [sb(f"rstd{k}", [P, TILES]) for k in range(2)]
        normed = [sb(f"normed{k}", [P, TILES, D]) for k in range(2)]
        x_hi = [sb(f"x_hi{k}", [P, KD, CHUNK], F16) for k in range(2)]
        x_lo = [sb(f"x_lo{k}", [P, KD, CHUNK], F16) for k in range(2)]
        forget = sb("forget", [P, KD, CHUNK])
        inp = sb("inp", [P, KD, CHUNK])
        cand_sig = sb("cand_sig", [P, KD, CHUNK])
        cand_lin = sb("cand_lin", [P, KD, CHUNK])
        cand = sb("cand", [P, KD, CHUNK])
        value = sb("value", [P, KD, CHUNK])
        hid = sb("hid", [P, KD, CHUNK])
        low = sb("low", [P, CHUNK], F16)
        relu = sb("relu", [P, 2, 2, CHUNK])
        sq = sb("sq", [P, 2, 2, CHUNK])
        sq_hi = sb("sq_hi", [P, FC, CHUNK], F16)
        sq_lo = sb("sq_lo", [P, FC, CHUNK], F16)
        y_sb = sb("y_sb", [P, TILES, D])
        out_sb = sb("out_sb", [P, 2, TILES, D])

        ids_sb = sb("ids_sb", [P, P], I32)
        ids_f = sb("ids_f", [P, 4, P])
        w_raw = sb("w_raw", [P, 6, D])
        w_max = sb("w_max", [P, 6])
        w_pow = sb("w_pow", [P, 6], I32)
        w_inv = sb("w_inv", [P, 6])
        fc_raw = sb("fc_raw", [P, FC, D])
        fc_a = sb("fc_a", [P, FC, D])
        fc_b = sb("fc_b", [P, FC, D])
        fc_s = sb("fc_s", [P, 3, FC])
        fc_inv = sb("fc_inv", [P, FC])
        pj_raw = sb("pj_raw", [P, KD, HID])
        pj_a = sb("pj_a", [P, KD, HID])
        pj_s = sb("pj_s", [P, 3, KD])
        pj_b = sb("pj_b", [P, KD, P])
        u_raw = sb("u_raw", [P, FC, R])
        u_0 = sb("u_0", [P, FC, R])
        u_1 = sb("u_1", [P, FC, R])
        u_hi = sb("u_hi", [P, FC, R], F16)
        u_parts = sb("u_parts", [P, FC, 2, 2, 2, R])
        u_sum = sb("u_sum", [P, FC])
        u_max = sb("u_max", [P, FC])
        u_pow = sb("u_pow", [P, FC], I32)
        u_inv = sb("u_inv", [P, FC])
        bound = sb("bound", [P, FC])
        bound_1 = sb("bound_1", [P, 1])
        bound_b = sb("bound_b", [P, P])
        bound_2 = sb("bound_2", [P, 1])
        bound_pow = sb("bound_pow", [P, 1], I32)
        shrink = sb("shrink", [P, 1])
        grow = sb("grow", [P, 1])
        gate_sb = sb("gate_sb", [P, 1])
        v_sb = sb("v_sb", [R, D])
        fb_sb = sb("fb_sb", [R, R])
        fb_t = sb("fb_t", [R, R])
        a_sb = sb("a_sb", [R, D])
        a_sq = sb("a_sq", [R, D])
        a_ss = sb("a_ss", [R, 1])
        a_norm = sb("a_norm", [R, 1])
        a_pow = sb("a_pow", [R, 1], I32)
        a_inv = sb("a_inv", [R, 1])
        a_nb = sb("a_nb", [R, P])
        plus_half = sb("plus_half", [R, 1])
        ones = sb("ones", [P, P])
        a_hi = sb("a_hi", [P, KD, R], F16)

        turned = ctx.enter_context(nc.psum_tensor("turned", [P, 1024], F32))
        y_ps = ctx.enter_context(nc.psum_tensor("y_ps", [P, TILES, D], F32))
        bank = [ctx.enter_context(nc.psum_tensor(f"bank{k}", [P, CHUNK], F32)) for k in range(4)]
        gate_bank = (0, 1, 2, 3, 1, 2)
        fc_bank = (3, 0, 1, 2, 3, 0, 1, 2)
        turned_cols = turned[:, :].rearrange("p (k t) -> p k t", k=KD)
        y_half = [y_ps[:, 2 * b:2 * b + 2, :].rearrange("p j d -> p (j d)") for b in range(2)]
        turned_rows = turned[:, :].rearrange("p (j d) -> p j d", j=TILES)

        ids_in, w_in, fc_in, pj_in, low_in = (sem(x) for x in ("ids_in", "w_in", "fc_in", "pj_in", "low_in"))
        blank_ready, ident_ready, consts_ready = sem("blank_ready"), sem("ident_ready"), sem("consts_ready")
        dve_chain = sem("dve_chain")
        ids_turned, idx_ready, ids_masked = sem("ids_turned"), sem("idx_ready"), sem("ids_masked")
        w_scaled, w_turned, w_hi_ready, w_lo_ready = (sem(x) for x in ("w_scaled", "w_turned", "w_hi_ready", "w_lo_ready"))
        fb_turned, fb_ready, a_ready, a_summed, a_rooted, a_scaled, a_turned, low_a_ready = (sem(x) for x in (
            "fb_turned", "fb_ready", "a_ready", "a_summed", "a_rooted", "a_scaled", "a_turned", "low_a_ready"))
        anorm_spread, bound_set, bound_spread, u_ready, u_turned, u_copied = (sem(x) for x in (
            "anorm_spread", "bound_set", "bound_spread", "u_ready", "u_turned", "u_copied"))
        abs_summed, fc_cut, pj_cut, scales_set = (sem(x) for x in ("abs_summed", "fc_cut", "pj_cut", "scales_set"))
        fc_ready, fc_turned, fc_copied, pj_ready, pj_turned, pj_copied, pj_spread = (sem(x) for x in (
            "fc_ready", "fc_turned", "fc_copied", "pj_ready", "pj_turned", "pj_copied", "pj_spread"))

        pool_passed, dve_passed = sem("pool_passed"), sem("dve_passed")
        raw_cleared = sem("raw_cleared")
        idx_set = sem("idx_set")
        gathered = [sem("gathered_even"), sem("gathered_odd")]
        raw_split = sem("raw_split")
        h0_ready = sem("h0_ready")
        stats_ready = [sem("stats_ready0"), sem("stats_ready1")]
        moments_ready = [sem("moments_ready0"), sem("moments_ready1")]
        var_ready = [sem("var_ready0"), sem("var_ready1")]
        rstd_ready = [sem("rstd_ready0"), sem("rstd_ready1")]
        normed_ready = [sem("normed_ready0"), sem("normed_ready1")]
        x_turned = [sem("x_turned0"), sem("x_turned1")]
        x_hi_ready = [sem("x_hi_ready0"), sem("x_hi_ready1")]
        x_lo_ready = [sem("x_lo_ready0"), sem("x_lo_ready1")]
        gate_done = sem("gate_done")
        gate_taken = sem("gate_taken")
        cand_ready = sem("cand_ready")
        value_ready = sem("value_ready")
        scanned = sem("scanned")
        hid_turned = sem("hid_turned")
        h1_ready = sem("h1_ready")
        low_done = sem("low_done")
        low_hi_ready = sem("low_hi_ready")
        low_ready = sem("low_ready")
        fc_done = sem("fc_done")
        relu_ready = sem("relu_ready")
        sq_ready = sem("sq_ready")
        sq_hi_ready = sem("sq_hi_ready")
        sq_lo_ready = sem("sq_lo_ready")
        y_done = sem("y_done")
        y_scaled = sem("y_scaled")
        out_ready = sem("out_ready")
        stored = [sem("stored_even"), sem("stored_odd")]

        def wait(eng, s, count):
            if not isinstance(count, int) or count > 0:
                eng.wait_ge(s, count)

        def pass_on(eng, passed, n):
            if not isinstance(n, int):
                eng.sem_inc(passed, 1)

        def steps(eng, step):
            for n in range(FIRST_LOOP):
                step(n, n // 2, n % 2)
            with eng.Fori(0, (LAST_LOOP + 1 - FIRST_LOOP) // 2) as i:
                step(i * 2 + FIRST_LOOP, i + FIRST_LOOP // 2, FIRST_LOOP % 2)
                step(i * 2 + FIRST_LOOP + 1, i + (FIRST_LOOP + 1) // 2, (FIRST_LOOP + 1) % 2)
            for n in range(LAST_LOOP + 1, N + 1):
                step(n, n // 2, n % 2)

        def known_below(n, limit):
            return not isinstance(n, int) or n < limit

        block = ctx.enter_context(nc.Block())

        @block.sync
        def _(sp):
            sp.dma_start(ids_sb[:, :], ids.rearrange("b (h p) -> (b h) p", p=P)).then_inc(ids_in, 16)
            for g, w in enumerate((wf, wi, wh)):
                sp.dma_start(w_raw[:, 2 * g:2 * g + 2, :], w.rearrange("(h p) d -> p h d", p=P)).then_inc(w_in, 16)
            sp.dma_start(v_sb[:, :], v[:, :]).then_inc(low_in, 16)
            sp.dma_start(fb_sb[:, :], fast_b[:, :]).then_inc(low_in, 16)
            sp.dma_start(gate_sb[:, :], gate.partition_broadcast(P)).then_inc(low_in, 16)
            sp.dma_start(u_raw[:, :, :], u.rearrange("(g p) r -> p g r", p=P)).then_inc(low_in, 16)
            sp.dma_start(fc_raw[:, :, :], w_fc.rearrange("(g p) d -> p g d", p=P)).then_inc(fc_in, 16)
            sp.dma_start(pj_raw[:, :, :], w_proj.rearrange("(g p) f -> p g f", p=P)).then_inc(pj_in, 16)

            def step(n, h, par):
                if isinstance(n, int) and n == 0:
                    return
                m, even = n - 1, 1 - par
                first = sp.snap(m * CHUNK) if not isinstance(m, int) else m * CHUNK
                sp.wait_ge(out_ready, m + 1)
                sp.dma_start(out[bass.ds(first, CHUNK), :].rearrange("(j p) d -> p j d", p=P),
                             out_sb[:, even, :, :]).then_inc(stored[even], 16)

            steps(sp, step)
            for s in stored:
                sp.wait_ge(s, 16 * (N // 2))

        @block.gpsimd
        def _(pool):
            pool.memset(ident[:, :], 0.0).then_inc(blank_ready, 1)
            pool.memset(minus_half[:, :], -0.5).then_inc(consts_ready, 1)
            pool.memset(plus_half[:, :], 0.5).then_inc(consts_ready, 1)
            pool.memset(ones[:, :], 1.0).then_inc(consts_ready, 1)
            pool.wait_ge(blank_ready, 1)
            pool.affine_select(out=ident[:, :], in_=ident[:, :], compare_op=ALU.not_equal, fill=1.0, base=0,
                               pattern=[[-1, P]], channel_multiplier=1).then_inc(ident_ready, 1)

            def gather(c, h, par):
                wait(pool, raw_split, 2 * (c - 1))
                pass_on(pool, pool_passed, c)
                pool.memset(rows_raw[:, par, :, :], 0.0).then_inc(raw_cleared, 1)
                pool.tensor_copy(idx_now[:, par, :], idx_all[:, bass.ds(c * TILES, TILES)]).then_inc(idx_set, 1)
                pool.wait_ge(raw_cleared, c + 1)
                pool.wait_ge(idx_set, c + 1)
                pass_on(pool, pool_passed, c)
                for j in range(TILES):
                    pool.indirect_dma_start(
                        rows_raw[:, par, j, :], None, table,
                        bass.IndirectOffsetOnAxis(ap=idx_now[:, par, j:j + 1], axis=0),
                        bounds_check=V - 1, oob_is_err=False).then_inc(gathered[par], 16)

            def root(k, c):
                pool.wait_ge(moments_ready[k], TILES * (c + 1))
                pass_on(pool, pool_passed, c)
                pool.tensor_scalar(var_eps[k][:, :], moments[k][:, :, 1], EPS, None, ALU.add)\
                    .then_inc(var_ready[k], 1)
                pool.wait_ge(var_ready[k], c + 1)
                pool.tensor_tensor(rstd[k][:, :], var_eps[k][:, :], minus_half[:, :], ALU.pow)\
                    .then_inc(rstd_ready[k], 1)

            pool.wait_ge(idx_ready, 1)
            pool.wait_ge(consts_ready, 3)
            gather(0, 0, 0)
            gather(1, 0, 1)
            root(0, 0)
            pool.wait_ge(a_summed, 1)
            pool.tensor_tensor(a_norm[:, :], a_ss[:, :], plus_half[:, :], ALU.pow).then_inc(a_rooted, 1)
            gather(2, 1, 0)

            def step(n, h, par):
                m = n - 1
                if known_below(n, N - 1):
                    root(0, n + 1)
                if known_below(n, N):
                    for e in range(KD):
                        pool.wait_ge(cand_ready, 2 * n + e + 1)
                        wait(pool, scanned, 4 * (n - 1) + 2 * e + 2)
                        pool.wait_ge(gate_taken, 8 * n + 4 * e + 4)
                        pool.tensor_tensor(value[:, e, :], inp[:, e, :], cand[:, e, :], ALU.mult)\
                            .then_inc(value_ready, 1)
                if isinstance(n, int) and n == 0:
                    for g in range(FC):
                        pool.wait_ge(fc_cut, 2 * g + 2)
                        pool.tensor_tensor(fc_b[:, g, :], fc_b[:, g, :], fc_a[:, g, :], ALU.subtract)\
                            .then_inc(fc_ready, 1)
                    root(1, n)
                if known_below(n, N - 3):
                    gather(n + 3, None, 1 - par)
                if not isinstance(n, int) or 0 < n < N:
                    root(1, n)
                if isinstance(n, int) and n == 0:
                    for k in range(KD):
                        pool.wait_ge(pj_cut, 2 * k + 2)
                        pool.tensor_tensor(pj_raw[:, k, :], pj_raw[:, k, :], pj_a[:, k, :], ALU.subtract)\
                            .then_inc(pj_ready, 1)
                if not isinstance(n, int) or n > 0:
                    wait(pool, stored[1 - par], (h if par else h - 1) * 16)
                    pool.wait_ge(h1_ready, m + 1)
                    pool.wait_ge(y_scaled, m + 1)
                    pool.tensor_tensor(out_sb[:, 1 - par, :, :], y_sb[:, :, :], h1[:, 1 - par, :, :], ALU.add)\
                        .then_inc(out_ready, 1)

            steps(pool, step)

        @block.scalar
        def _(act):
            for b in range(3):
                act.wait_ge(w_turned, b + 1)
                act.activation(w_hi[:, :, :, :].rearrange("p k g e -> p (k g e)")[:, b * 512:(b + 1) * 512],
                               bank[b][:, :], ACT.Copy).then_inc(w_hi_ready, 1)

            act.wait_ge(fc_in, 16)
            for g in range(FC):
                act.activation(fc_a[:, g, :], fc_raw[:, g, :], ACT.Abs, accum_out=fc_s[:, 0, g:g + 1])\
                    .then_inc(abs_summed, 1)
            act.wait_ge(pj_in, 16)
            for k in range(KD):
                act.activation(pj_a[:, k, :], pj_raw[:, k, :], ACT.Abs, accum_out=pj_s[:, 0, k:k + 1])\
                    .then_inc(abs_summed, 1)

            def x_high(k, c):
                act.wait_ge(x_turned[k], c + 1)
                act.activation(x_hi[k][:, :, :], turned_cols, ACT.Copy).then_inc(x_hi_ready[k], 1)

            x_high(0, 0)

            def low_high(m):
                act.wait_ge(low_done, m + 1)
                wait(act, fc_done, FC * m)
                act.activation(low[:, :], bank[0][:, :], ACT.Copy).then_inc(low_hi_ready, 1)

            def copy_fc(b):
                k, g = divmod(4 * b, FC)
                act.wait_ge(fc_turned, b + 1)
                act.activation(fc_t[:, k, g * P:(g + 4) * P], y_half[0], ACT.Copy).then_inc(fc_copied, 1)

            def copy_proj(b):
                act.wait_ge(pj_turned, b + 1)
                act.activation(proj_t[:, 2 * b:2 * b + 2, :], y_ps[:, 2 * (b % 2):2 * (b % 2) + 2, :], ACT.Copy)\
                    .then_inc(pj_copied, 1)

            def step(n, h, par):
                m = n - 1
                front = known_below(n, N)
                back = not isinstance(n, int) or n > 0
                def columns():
                    wait(act, fc_done, FC * m)
                    x_high(1, m)

                if back and not front:
                    columns()
                if front:
                    for e in range(KD):
                        for q, (dst, func, bias) in enumerate((
                                (forget, ACT.Sigmoid, 0.0), (inp, ACT.Sigmoid, 0.0),
                                (cand_sig, ACT.Sigmoid, 0.0), (cand_lin, ACT.Identity, 0.5))):
                            g = min(q, 2)
                            act.wait_ge(gate_done, 6 * n + 3 * e + g + 1)
                            if q == 0:
                                wait(act, scanned, 4 * (n - 1) + 2 * e + 2)
                            if q == 1:
                                wait(act, value_ready, 2 * (n - 1) + e + 1)
                            if q >= 2:
                                wait(act, cand_ready, 2 * (n - 1) + e + 1)
                            act.activation(dst[:, e, :], bank[gate_bank[3 * e + g]][:, :], func, bias=bias,
                                           scale=w_back[:, 2 * g + e:2 * g + e + 1]).then_inc(gate_taken, 1)
                            if back and (e, q) == (0, 1):
                                columns()
                            if isinstance(n, int) and n == 1 and (e, q) in ((0, 3), (1, 0), (1, 1), (1, 3)):
                                copy_fc(((0, 3), (1, 0), (1, 1), (1, 3)).index((e, q)))
                            if back and (e, q) == (1, 0):
                                low_high(m)
                elif back:
                    low_high(m)
                if isinstance(n, int) and n == 1:
                    for b in range(2):
                        act.wait_ge(u_turned, b + 1)
                        act.activation(low_u[:, b * 512:(b + 1) * 512], y_half[b], ACT.Copy)\
                            .then_inc(u_copied, 1)
                for p in range(FC // 2):
                    if back:
                        for f in (2 * p, 2 * p + 1):
                            act.wait_ge(fc_done, FC * m + f + 1)
                            wait(act, sq_ready, 4 * m + p - 1)
                            act.activation(relu[:, p % 2, f % 2, :], bank[fc_bank[f]][:, :], ACT.Relu,
                                           scale=relu_scale[:, f:f + 1]).then_inc(relu_ready, 1)
                        act.wait_ge(relu_ready, FC * m + 2 * p + 2)
                        wait(act, sq_lo_ready, 4 * m + p - 1)
                        act.activation(sq[:, p % 2, :, :], relu[:, p % 2, :, :], ACT.Square)\
                            .then_inc(sq_ready, 1)
                    if p == 1 and known_below(n, N - 1):
                        act.wait_ge(gate_done, 6 * (n + 1))
                        x_high(0, n + 1)
                    if isinstance(n, int) and n == 1:
                        for b in ((0,), (1,), (2, 3), ())[p]:
                            copy_proj(b)

            steps(act, step)

        @block.tensor
        def _(pe):
            pe.wait_ge(ident_ready, 1)
            pe.wait_ge(ids_masked, 1)
            pe.transpose(y_ps[:, 0, 0:P], ids_f[:, 3, :], ident[:, :]).then_inc(ids_turned, 1)
            pe.wait_ge(w_scaled, 1)
            for b in range(3):
                for q in range(4):
                    k, g = divmod(4 * b + q, 6)
                    ins = pe.transpose(bank[b][:, q * P:(q + 1) * P], w_raw[:, g, k * P:(k + 1) * P], ident[:, :])
                ins.then_inc(w_turned, 1)
            pe.wait_ge(low_in, 64)
            pe.transpose(bank[3][0:R, 0:R], fb_sb[:, :], ident[0:R, 0:R]).then_inc(fb_turned, 1)
            pe.wait_ge(fb_ready, 1)
            pe.matmul(y_ps[0:R, 1, :], fb_t[:, :], v_sb[:, :], start=True, stop=True).then_inc(a_ready, 1)
            pe.wait_ge(a_scaled, 2)
            for k in range(KD):
                pe.transpose(bank[3][:, 128 + k * R:128 + (k + 1) * R], a_sb[:, k * P:(k + 1) * P], ident[0:R, 0:R])\
                    .then_inc(a_turned, 1)
            pe.matmul(y_ps[:, 2, 0:R], a_nb[:, :], ident[0:R, 0:R], start=True, stop=True).then_inc(anorm_spread, 1)

            def turn(k, c):
                pe.wait_ge(normed_ready[k], TILES * (c + 1))
                for e in range(KD):
                    for j in range(TILES):
                        ins = pe.transpose(turned_cols[:, e, j * P:(j + 1) * P],
                                           normed[k][:, j, e * P:(e + 1) * P], ident[:, :])
                ins.then_inc(x_turned[k], 1)

            turn(0, 0)
            def turn_bound():
                pe.wait_ge(bound_set, 1)
                pe.transpose(y_ps[:, 2, P:D], bound_b[:, :], ident[:, :]).then_inc(bound_spread, 1)

            def spread_proj_scale():
                pe.wait_ge(scales_set, KD)
                for k in range(KD):
                    ins = pe.matmul(y_ps[:, 3, k * P:(k + 1) * P], pj_b[:, k, :], ident[:, :], start=True, stop=True)
                ins.then_inc(pj_spread, 1)

            def turn_fc(b):
                if b > 0:
                    pe.wait_ge(fc_copied, b)
                for q in range(4):
                    k, g = divmod(4 * b + q, FC)
                    pe.wait_ge(fc_ready, g + 1)
                    ins = pe.transpose(y_half[0][:, q * P:(q + 1) * P], fc_b[:, g, k * P:(k + 1) * P], ident[:, :])
                ins.then_inc(fc_turned, 1)

            def turn_u():
                pe.wait_ge(u_ready, 1)
                pe.wait_ge(fc_copied, 4)
                for b in range(2):
                    for q in range(4):
                        ins = pe.transpose(y_half[b][:, q * P:(q + 1) * P],
                                           u_parts[:, 4 * b + q, :, :, :, :].rearrange("p a b c r -> p (a b c r)"),
                                           ident[:, :])
                    ins.then_inc(u_turned, 1)

            def turn_proj(b):
                pe.wait_ge(pj_ready, KD)
                if b < 2:
                    pe.wait_ge(u_copied, 2)
                else:
                    pe.wait_ge(pj_copied, b - 1)
                for f in range(2):
                    for k in range(KD):
                        ins = pe.transpose(y_ps[:, 2 * (b % 2) + f, k * P:(k + 1) * P],
                                           pj_raw[:, k, (2 * b + f) * P:(2 * b + f + 1) * P], ident[:, :])
                ins.then_inc(pj_turned, 1)

            def low_rank(n, m, front):
                pe.wait_ge(x_hi_ready[1], m + 1)
                pe.wait_ge(x_lo_ready[1], m + 1)
                if front:
                    pe.wait_ge(gate_taken, 8 * n + 1)
                else:
                    pe.wait_ge(relu_ready, FC * (n - 2) + 6)
                for k in range(KD):
                    pe.matmul(bank[0][:, :], low_a[:, k, :], x_hi[1][:, k, :], start=(k == 0), stop=False)
                    ins = pe.matmul(bank[0][:, :], low_a[:, k, :], x_lo[1][:, k, :], start=False, stop=(k == KD - 1))
                ins.then_inc(low_done, 1)

            def step(n, h, par):
                m = n - 1
                front = known_below(n, N)
                back = not isinstance(n, int) or n > 0
                if front:
                    pe.wait_ge(x_hi_ready[0], n + 1)
                    pe.wait_ge(x_lo_ready[0], n + 1)
                    for p in range(6):
                        e, g = divmod(p, 3)
                        if p < 4:
                            wait(pe, relu_ready, FC * (n - 2) + (6, 7, 8, 5)[p])
                            if isinstance(n, int) and n == 1:
                                pe.wait_ge(gate_taken, 8)
                            if isinstance(n, int) and n == 0:
                                if p < 3:
                                    pe.wait_ge(w_lo_ready, 3)
                                else:
                                    pe.wait_ge(low_a_ready, 1)
                        else:
                            pe.wait_ge(gate_taken, 8 * n + (2, 4)[p - 4])
                        q = 2 * g + e
                        for k in range(KD):
                            for w in (w_hi, w_lo):
                                for x in (x_hi, x_lo):
                                    ins = pe.matmul(bank[gate_bank[p]][:, :], w[:, k, q, :], x[0][:, k, :],
                                                    start=(k == 0 and w is w_hi and x is x_hi),
                                                    stop=(k == KD - 1 and w is w_lo and x is x_lo))
                        ins.then_inc(gate_done, 1)
                        if back and p == 1:
                            pe.wait_ge(h1_ready, n)
                            turn(1, m)
                        if back and p == 3:
                            low_rank(n, m, True)
                        if isinstance(n, int) and n == 1 and p >= 2:
                            turn_fc(p - 2)
                elif back:
                    pe.wait_ge(h1_ready, n)
                    turn(1, m)
                    low_rank(n, m, False)
                if isinstance(n, int) and n == 0:
                    turn_bound()
                    spread_proj_scale()
                if isinstance(n, int) and n == 1:
                    turn_u()
                    pe.wait_ge(u_copied, 2)
                    pe.wait_ge(u_ready, 1)
                for f in range(FC):
                    if back:
                        if f == 1:
                            pe.wait_ge(low_ready, m + 1)
                            pe.wait_ge(low_hi_ready, m + 1)
                        elif f > 3:
                            pe.wait_ge(relu_ready, FC * m + f - 3)
                        elif front:
                            pe.wait_ge(gate_taken, 8 * n + (5, 0, 6, 8)[f])
                        else:
                            pe.wait_ge(relu_ready, FC * (n - 2) + (5, 0, 7, 8)[f])
                        dst = bank[fc_bank[f]]
                        for k in range(KD):
                            pe.matmul(dst[:, :], fc_t[:, k, f * P:(f + 1) * P], x_hi[1][:, k, :],
                                      start=(k == 0), stop=False)
                            pe.matmul(dst[:, :], fc_t[:, k, f * P:(f + 1) * P], x_lo[1][:, k, :],
                                      start=False, stop=False)
                        if f == 0:
                            pe.wait_ge(low_ready, m + 1)
                        pe.matmul(dst[:, :], low_u[:, f * P:(f + 1) * P], low[:, :], start=False, stop=True)\
                            .then_inc(fc_done, 1)
                    if f == 3 and known_below(n, N - 1):
                        wait(pe, x_hi_ready[1], n)
                        wait(pe, x_lo_ready[1], n)
                        turn(0, n + 1)
                    if isinstance(n, int) and n == 1 and f in (1, 2, 4, 5):
                        turn_proj((1, 2, 4, 5).index(f))
                if front:
                    pe.wait_ge(scanned, 4 * (n + 1))
                    ahead = min(n + 2, N) if isinstance(n, int) else n + 2
                    pe.wait_ge(x_hi_ready[0], ahead)
                    pe.wait_ge(x_lo_ready[0], ahead)
                    for j in range(TILES):
                        for e in range(KD):
                            ins = pe.transpose(turned_rows[:, j, e * P:(e + 1) * P],
                                               hid[:, e, j * P:(j + 1) * P], ident[:, :])
                    ins.then_inc(hid_turned, 1)
                if back:
                    wait(pe, y_scaled, m)
                    if isinstance(n, int) and n == 1:
                        pe.wait_ge(pj_copied, 4)
                    for f in range(FC):
                        if f % 2 == 0:
                            pe.wait_ge(sq_hi_ready, 4 * m + f // 2 + 1)
                            pe.wait_ge(sq_lo_ready, 4 * m + f // 2 + 1)
                        for j in range(TILES):
                            for part in (sq_hi, sq_lo):
                                ins = pe.matmul(y_ps[:, j, :], part[:, f, j * P:(j + 1) * P], proj_t[:, f, :],
                                                start=(f == 0 and j % 2 == 0 and part is sq_hi),
                                                stop=(f == FC - 1 and part is sq_lo), skip_group_check=True)
                    ins.then_inc(y_done, 1)

            steps(pe, step)

        @block.vector
        def _(dve):
            chain = [0]

            def mark(ins):
                chain[0] += 1
                return ins.then_inc(dve_chain, 1)

            def settle():
                dve.wait_ge(dve_chain, chain[0])

            dve.wait_ge(ids_in, 16)
            mark(dve.tensor_copy(ids_f[:, 0, :], ids_sb[:, :]))
            settle()
            mark(dve.tensor_scalar(ids_f[:, 1, :], ids_f[:, 0, :], 0.0, float(V), ALU.is_lt, ALU.mult))
            settle()
            mark(dve.tensor_tensor(ids_f[:, 0, :], ids_f[:, 0, :], ids_f[:, 1, :], ALU.add))
            settle()
            mark(dve.tensor_scalar(ids_f[:, 1, :], ids_f[:, 0, :], 0.0, None, ALU.is_ge))
            settle()
            mark(dve.scalar_tensor_tensor(ids_f[:, 2, :], ids_f[:, 0, :], float(V), ids_f[:, 1, :], ALU.is_lt, ALU.mult))
            settle()
            mark(dve.scalar_tensor_tensor(ids_f[:, 1, :], ids_f[:, 0, :], -float(V), ids_f[:, 2, :], ALU.add, ALU.mult))
            settle()
            dve.tensor_scalar(ids_f[:, 3, :], ids_f[:, 1, :], float(V), None, ALU.add).then_inc(ids_masked, 1)
            dve.wait_ge(ids_turned, 1)
            dve.tensor_copy(idx_all[:, :], y_ps[:, 0, 0:P]).then_inc(idx_ready, 1)

            dve.wait_ge(w_in, 48)
            mark(dve.tensor_reduce(w_max[:, :], w_raw[:, :, :], AX, ALU.max, apply_absolute_value=True))
            settle()
            mark(dve.tensor_scalar(w_max[:, :], w_max[:, :], 2.0 ** -60, None, ALU.max))
            settle()
            mark(dve.tensor_scalar(w_pow[:, :], w_max[:, :].bitcast(I32), EXPONENT, None, ALU.bitwise_and))
            settle()
            mark(dve.tensor_scalar(w_back[:, :], w_pow[:, :].bitcast(F32), 1 / W_TOP, None, ALU.mult))
            settle()
            mark(dve.reciprocal(w_inv[:, :], w_back[:, :]))
            settle()
            for g in range(6):
                ins = mark(dve.tensor_scalar(w_raw[:, g, :], w_raw[:, g, :], w_inv[:, g:g + 1], None, ALU.mult))
            settle()
            dve.tensor_copy(w_max[:, 0:1], w_inv[:, 0:1]).then_inc(w_scaled, 1)

            dve.wait_ge(fb_turned, 1)
            dve.tensor_copy(fb_t[:, :], bank[3][0:R, 0:R]).then_inc(fb_ready, 1)
            dve.wait_ge(a_ready, 1)
            mark(dve.tensor_copy(a_sb[:, :], y_ps[0:R, 1, :]))
            settle()
            mark(dve.tensor_tensor(a_sq[:, :], a_sb[:, :], a_sb[:, :], ALU.mult))
            settle()
            dve.tensor_reduce(a_ss[:, :], a_sq[:, :], AX, ALU.add).then_inc(a_summed, 1)

            for b in range(3):
                dve.wait_ge(w_hi_ready, b + 1)
                whole = [w[:, :, :, :].rearrange("p k g e -> p (k g e)")[:, b * 512:(b + 1) * 512] for w in (w_hi, w_lo)]
                dve.tensor_tensor(whole[1], bank[b][:, :], whole[0], ALU.subtract).then_inc(w_lo_ready, 1)

            def guard(c, wait_h, par):
                dve.wait_ge(gathered[par], wait_h)
                wait(dve, h0_ready, c)
                dve.tensor_scalar(rows_pos[:, :, :], rows_raw[:, par, :, :], 0.0, FMAX, ALU.max, ALU.min)\
                    .then_inc(raw_split, 1)
                dve.tensor_scalar(rows_neg[:, :, :], rows_raw[:, par, :, :], 0.0, -FMAX, ALU.min, ALU.max)\
                    .then_inc(raw_split, 1)

            def guard_sum(c, par):
                dve.wait_ge(raw_split, 2 * (c + 1))
                dve.tensor_tensor(h0[:, par, :, :], rows_pos[:, :, :], rows_neg[:, :, :], ALU.add).then_inc(h0_ready, 1)

            def measure(k, c, rows):
                for j in range(TILES):
                    dve.bn_stats(stats[k][:, j, :], rows[:, j, :]).then_inc(stats_ready[k], 1)
                dve.wait_ge(stats_ready[k], TILES * (c + 1))
                pass_on(dve, dve_passed, c)
                for j in range(TILES):
                    dve.bn_aggr(moments[k][:, j, :], stats[k][:, j, :]).then_inc(moments_ready[k], 1)

            def normalise(k, c, rows):
                dve.wait_ge(rstd_ready[k], c + 1)
                wait(dve, x_turned[k], c)
                for j in range(TILES):
                    dve.tensor_scalar(normed[k][:, j, :], rows[:, j, :], moments[k][:, j, 0:1],
                                      rstd[k][:, j:j + 1], ALU.subtract, ALU.mult).then_inc(normed_ready[k], 1)

            def x_low(k, c):
                dve.wait_ge(x_hi_ready[k], c + 1)
                dve.tensor_tensor(x_lo[k][:, :, :], turned_cols, x_hi[k][:, :, :], ALU.subtract)\
                    .then_inc(x_lo_ready[k], 1)

            def scale_low_rank():
                dve.wait_ge(a_rooted, 1)
                mark(dve.tensor_scalar(a_norm[:, :], a_norm[:, :], 2.0 ** -60, None, ALU.max))
                settle()
                mark(dve.tensor_scalar(a_pow[:, :], a_norm[:, :].bitcast(I32), EXPONENT, None, ALU.bitwise_and))
                settle()
                mark(dve.reciprocal(a_inv[:, :], a_pow[:, :].bitcast(F32)))
                settle()
                dve.wait_ge(consts_ready, 3)
                dve.tensor_scalar(a_sb[:, :], a_sb[:, :], a_inv[:, :], LOW_TOP, ALU.mult, ALU.mult).then_inc(a_scaled, 1)
                dve.tensor_scalar(a_nb[:, :], ones[0:R, :], a_pow[:, :].bitcast(F32), None, ALU.mult).then_inc(a_scaled, 1)

            def split_low_rank():
                dve.wait_ge(a_turned, KD)
                a_cols = bank[3][:, 128:128 + KD * R].rearrange("p (k r) -> p k r", k=KD)
                mark(dve.tensor_copy(a_hi[:, :, :], a_cols))
                settle()
                low_av = low_a[:, :, :].rearrange("p k (s a u r) -> p k s a u r", s=2, a=2, u=2)
                for s in range(2):
                    for q in range(2):
                        mark(dve.tensor_copy(low_av[:, :, s, 0, q, :], a_hi[:, :, :]))
                        mark(dve.tensor_tensor(low_av[:, :, s, 1, q, :], a_cols, a_hi[:, :, :], ALU.subtract))
                settle()
                dve.tensor_copy(a_nb[:, 0:1], a_inv[:, :]).then_inc(low_a_ready, 1)

            def over_rank(column):
                return column.unsqueeze(2).to_broadcast([P, FC, R])

            def prepare_scales():
                dve.wait_ge(abs_summed, FC + KD)
                mark(dve.tensor_scalar(fc_s[:, 0, :], fc_s[:, 0, :], 1 / D, 1e-5, ALU.mult, ALU.max))
                mark(dve.tensor_scalar(pj_s[:, 0, :], pj_s[:, 0, :], 1 / HID, 1e-5, ALU.mult, ALU.max))
                dve.wait_ge(anorm_spread, 1)
                dve.wait_ge(low_in, 64)
                mark(dve.scalar_tensor_tensor(u_0[:, :, :], u_raw[:, :, :], gate_sb[:, :],
                                              y_ps[:, 2, 0:R].unsqueeze(1).to_broadcast([P, FC, R]),
                                              ALU.mult, ALU.mult))
                settle()
                for q, half in ((1, 0.5), (2, -0.5)):
                    mark(dve.tensor_scalar(fc_s[:, q, :], fc_s[:, 0, :], half, None, ALU.mult))
                    mark(dve.tensor_scalar(pj_s[:, q, :], pj_s[:, 0, :], half, None, ALU.mult))
                mark(dve.reciprocal(fc_inv[:, :], fc_s[:, 0, :]))
                mark(dve.tensor_reduce(u_sum[:, :], u_0[:, :, :], AX, ALU.add, apply_absolute_value=True))
                settle()
                mark(dve.tensor_scalar(bound[:, :], u_sum[:, :], 32.0, None, ALU.mult))
                mark(dve.tensor_tensor(u_1[:, :, :], u_0[:, :, :], over_rank(fc_inv[:, :]), ALU.mult))
                settle()
                mark(dve.scalar_tensor_tensor(bound[:, :], fc_s[:, 0, :], 256.0, bound[:, :], ALU.mult, ALU.add))
                mark(dve.tensor_reduce(u_max[:, :], u_1[:, :, :], AX, ALU.max, apply_absolute_value=True))
                settle()
                mark(dve.tensor_reduce(bound_1[:, :], bound[:, :], AX, ALU.max))
                mark(dve.tensor_scalar(u_max[:, :], u_max[:, :], 1 / LOW_TOP, 2.0 ** -10, ALU.mult, ALU.max))
                settle()
                dve.tensor_scalar(bound_b[:, :], ones[:, :], bound_1[:, :], None, ALU.mult).then_inc(bound_set, 1)
                mark(dve.tensor_scalar(u_pow[:, :], u_max[:, :].bitcast(I32), EXPONENT, None, ALU.bitwise_and))
                settle()
                mark(dve.tensor_scalar(u_max[:, :], u_pow[:, :].bitcast(F32), 1 / LOW_TOP, None, ALU.mult))
                settle()
                mark(dve.reciprocal(u_inv[:, :], u_max[:, :]))
                settle()
                for k in range(KD):
                    dve.tensor_scalar(pj_b[:, k, :], ones[:, :], pj_s[:, 0, k:k + 1], None, ALU.mult)\
                        .then_inc(scales_set, 1)

            def cut_fc():
                for g in range(FC):
                    for side, q, beyond in ((fc_a, 2, ALU.is_lt), (fc_b, 1, ALU.is_gt)):
                        dve.tensor_scalar(side[:, g, :], fc_raw[:, g, :], fc_s[:, q, g:g + 1], u_inv[:, g:g + 1],
                                          beyond, ALU.mult).then_inc(fc_cut, 1)

            def split_u():
                mark(dve.scalar_tensor_tensor(u_1[:, :, :], u_1[:, :, :], 1 / LOW_TOP, over_rank(u_inv[:, :]),
                                              ALU.mult, ALU.mult))
                settle()
                mark(dve.tensor_copy(u_hi[:, :, :], u_1[:, :, :]))
                settle()
                for q in range(4):
                    mark(dve.tensor_copy(u_parts[:, :, q // 2, q % 2, 0, :], u_hi[:, :, :]))
                    mark(dve.tensor_tensor(u_parts[:, :, q // 2, q % 2, 1, :], u_1[:, :, :], u_hi[:, :, :], ALU.subtract))
                dve.wait_ge(bound_spread, 1)
                mark(dve.tensor_reduce(bound_2[:, :], y_ps[:, 2, P:D], AX, ALU.max))
                settle()
                mark(dve.tensor_scalar(bound_pow[:, :], bound_2[:, :].bitcast(I32), EXPONENT, None, ALU.bitwise_and))
                settle()
                mark(dve.tensor_scalar(grow[:, :], bound_pow[:, :].bitcast(F32), 1 / RELU_TOP, None, ALU.mult))
                settle()
                mark(dve.reciprocal(shrink[:, :], grow[:, :]))
                mark(dve.tensor_tensor(relu_scale[:, :], fc_s[:, 0, :], u_max[:, :], ALU.mult))
                settle()
                mark(dve.tensor_scalar(relu_scale[:, :], relu_scale[:, :], shrink[:, :], None, ALU.mult))
                mark(dve.tensor_tensor(grow[:, :], grow[:, :], grow[:, :], ALU.mult))
                settle()
                dve.wait_ge(pj_spread, 1)
                dve.tensor_scalar(proj_scale[:, :], y_ps[:, 3, :], grow[:, :], None, ALU.mult).then_inc(u_ready, 1)

            def cut_proj():
                for k in range(KD):
                    dve.tensor_scalar(pj_a[:, k, :], pj_raw[:, k, :], pj_s[:, 2, k:k + 1], None, ALU.is_lt)\
                        .then_inc(pj_cut, 1)
                    dve.tensor_scalar(pj_raw[:, k, :], pj_raw[:, k, :], pj_s[:, 1, k:k + 1], None, ALU.is_gt)\
                        .then_inc(pj_cut, 1)

            guard(0, 64, 0)
            guard_sum(0, 0)
            dve.wait_ge(h0_ready, 1)
            measure(0, 0, h0[:, 0, :, :])
            normalise(0, 0, h0[:, 0, :, :])
            scale_low_rank()
            x_low(0, 0)
            split_low_rank()
            guard(1, 64, 1)
            guard_sum(1, 1)

            def step(n, h, par):
                m = n - 1
                front = known_below(n, N)
                back = not isinstance(n, int) or n > 0
                def x_low_1(m):
                    wait(dve, fc_done, FC * m)
                    x_low(1, m)

                if known_below(n, N - 1):
                    dve.wait_ge(h0_ready, n + 2)
                    measure(0, n + 1, h0[:, 1 - par, :, :])
                if isinstance(n, int) and n == 0:
                    prepare_scales()
                if back:
                    x_low_1(m)

                def candidate(e):
                    dve.wait_ge(gate_taken, 8 * n + 4 * e + 4)
                    wait(dve, value_ready, 2 * (n - 1) + e + 1)
                    dve.tensor_tensor(cand[:, e, :], cand_lin[:, e, :], cand_sig[:, e, :], ALU.max)\
                        .then_inc(cand_ready, 1)

                def scan(e):
                    dve.wait_ge(value_ready, 2 * n + e + 1)
                    wait(dve, hid_turned, n)
                    for s in range(CHUNK // T):
                        at = slice(s * T, (s + 1) * T)
                        dve.tensor_tensor_scan(hid[:, e, at], forget[:, e, at], value[:, e, at], 0.5,
                                               ALU.mult, ALU.add).then_inc(scanned, 1)

                if front:
                    candidate(0)
                if known_below(n, N - 1):
                    normalise(0, n + 1, h0[:, 1 - par, :, :])
                if front:
                    scan(0)
                if isinstance(n, int) and n == 0:
                    cut_fc()
                if back:
                    dve.wait_ge(low_hi_ready, m + 1)
                    dve.tensor_tensor(low[64:P, :], bank[0][64:P, :], low[64:P, :], ALU.subtract)\
                        .then_inc(low_ready, 1)
                if known_below(n, N - 2):
                    guard(n + 2, 64 * (h + 2), par)
                if front:
                    candidate(1)
                if front:
                    scan(1)
                for p in range(FC // 2):
                    if back:
                        dve.wait_ge(sq_ready, 4 * m + p + 1)
                        wait(dve, y_done, m)
                        dve.tensor_copy(sq_hi[:, 2 * p:2 * p + 2, :], sq[:, p % 2, :, :]).then_inc(sq_hi_ready, 1)
                        dve.wait_ge(sq_hi_ready, 4 * m + p + 1)
                        dve.tensor_tensor(sq_lo[:, 2 * p:2 * p + 2, :], sq[:, p % 2, :, :],
                                          sq_hi[:, 2 * p:2 * p + 2, :], ALU.subtract).then_inc(sq_lo_ready, 1)
                    if p == 1 and known_below(n, N - 1):
                        dve.wait_ge(gate_done, 6 * (n + 1))
                        x_low(0, n + 1)
                if front:
                    dve.wait_ge(hid_turned, n + 1)
                    wait(dve, out_ready, n - 1)
                    dve.tensor_tensor(h1[:, par, :, :], turned_rows, h0[:, par, :, :], ALU.add).then_inc(h1_ready, 1)
                    dve.wait_ge(h1_ready, n + 1)
                    measure(1, n, h1[:, par, :, :])
                if known_below(n, N - 2):
                    guard_sum(n + 2, par)
                if front:
                    normalise(1, n, h1[:, par, :, :])
                if isinstance(n, int) and n == 0:
                    split_u()
                    cut_proj()
                if back:
                    dve.wait_ge(y_done, m + 1)
                    wait(dve, out_ready, m)
                    dve.wait_ge(u_ready, 1)
                    dve.tensor_tensor(y_sb[:, :, :], y_ps[:, :, :],
                                      proj_scale[:, :].unsqueeze(1).to_broadcast([P, TILES, D]), ALU.mult)\
                        .then_inc(y_scaled, 1)

            steps(dve, step)


def kernel(x, L0_tok_embed_table, L0_attn_Wf, L0_attn_Wi, L0_attn_Wh, L0_ffn_fast_b, L0_ffn_w_fc, L0_ffn_w_proj,
           L0_ffn_u, L0_ffn_v, L0_ffn_gate):
    import numpy as np
    import concourse.bacc as bacc
    from concourse.bass_utils import run_bass_kernel_spmd

    nc = bacc.Bacc("TRN2", target_bir_lowering=False, num_devices=1)
    given = {
        "ids": x, "table": L0_tok_embed_table, "wf": L0_attn_Wf, "wi": L0_attn_Wi, "wh": L0_attn_Wh,
        "fast_b": L0_ffn_fast_b, "w_fc": L0_ffn_w_fc, "w_proj": L0_ffn_w_proj, "u": L0_ffn_u, "v": L0_ffn_v,
        "gate": np.asarray(L0_ffn_gate).reshape(1, 1),
    }
    arrays = {name: np.ascontiguousarray(a) for name, a in given.items()}
    aps = [nc.dram_tensor(name, a.shape, mybir.dt.from_np(a.dtype), kind="ExternalInput").ap()
           for name, a in arrays.items()]
    out = nc.dram_tensor("out", (SEQS * T, D), F32, kind="ExternalOutput").ap()
    build(nc, *aps, out)
    result = run_bass_kernel_spmd(nc, [arrays], core_ids=[0])
    return result.results[0]["out"].reshape(SEQS, T, D)
```
